# Optimizing a Trainium2 kernel written in Bass

```python
import numpy as np
import jax
import jax.numpy as jnp

def _softmax(x, axis=-1):
    return jax.nn.softmax(x, axis=axis)
def _gelu(x):
    return jax.nn.gelu(x, approximate=True)
def _silu(x):
    return jax.nn.silu(x)
def _sigmoid(x):
    return jax.nn.sigmoid(x)
def _layernorm(x, axis=-1, eps=1e-5):
    m = jnp.mean(x, axis=axis, keepdims=True)
    v = jnp.var(x, axis=axis, keepdims=True)
    return (x - m) / jnp.sqrt(v + eps)
def _scatter_add(tgt, idx, src, axis=0):
    return tgt.at[idx].add(src)
def _segment_sum(src, seg, n):
    return jax.ops.segment_sum(src, seg, n)

kernel_name = 'mk_conv_seq_d1_conv_nhwc192_e599f2'

def setup_inputs(seed: int = 0):
    np.random.seed(seed)
    _w = jnp.asarray
    def _rec_inputs():
        import jax
        import jax.numpy as jnp
        _gk = jax.random.key(seed)
        x = 7.572e-06 + 1 * jax.random.normal(jax.random.fold_in(_gk, 1), (16, 56, 56, 192), jnp.float32)
        return x
    x = _rec_inputs()
    def _L0_conv_setup():
        import jax, jax.numpy as jnp
        import numpy as np
        WS = 7
        SHIFT = 3
        NH = 6

        def layernorm(x, w, b, eps=1e-05):
            mu = jnp.mean(x, axis=-1, keepdims=True)
            var = jnp.var(x, axis=-1, keepdims=True)
            return (x - mu) * jax.lax.rsqrt(var + eps) * w + b
        key = jax.random.key(seed)
        ks = jax.random.split(key, 8)
        B, H, W, C = (16, 56, 56, 192)
        hid = 4 * C
        s = lambda k, shape, fan: jax.random.normal(k, shape, jnp.float32) * fan ** (-0.5)
        return {'x': jax.random.normal(ks[0], (B, H, W, C), jnp.float32), 'ln1_w': jnp.ones((C,), jnp.float32), 'ln1_b': jnp.zeros((C,), jnp.float32), 'qkv_w': s(ks[1], (C, 3 * C), C), 'qkv_b': jnp.zeros((3 * C,), jnp.float32), 'proj_w': s(ks[2], (C, C), C), 'proj_b': jnp.zeros((C,), jnp.float32), 'ln2_w': jnp.ones((C,), jnp.float32), 'ln2_b': jnp.zeros((C,), jnp.float32), 'mlp_w1': s(ks[3], (C, hid), C), 'mlp_b1': jnp.zeros((hid,), jnp.float32), 'mlp_w2': s(ks[4], (hid, C), hid), 'mlp_b2': jnp.zeros((C,), jnp.float32)}
    _L0_conv_all = _L0_conv_setup()
    _L0_conv_in = {k: v for k, v in _L0_conv_all.items() if k in ('ln1_w', 'ln1_b', 'qkv_w', 'qkv_b', 'proj_w', 'proj_b', 'ln2_w', 'ln2_b', 'mlp_w1', 'mlp_b1', 'mlp_w2', 'mlp_b2', )}
    del _L0_conv_all

    return {
        "x": x,
        "L0_conv_ln1_w": _L0_conv_in["ln1_w"],
        "L0_conv_ln1_b": _L0_conv_in["ln1_b"],
        "L0_conv_qkv_w": _L0_conv_in["qkv_w"],
        "L0_conv_qkv_b": _L0_conv_in["qkv_b"],
        "L0_conv_proj_w": _L0_conv_in["proj_w"],
        "L0_conv_proj_b": _L0_conv_in["proj_b"],
        "L0_conv_ln2_w": _L0_conv_in["ln2_w"],
        "L0_conv_ln2_b": _L0_conv_in["ln2_b"],
        "L0_conv_mlp_w1": _L0_conv_in["mlp_w1"],
        "L0_conv_mlp_b1": _L0_conv_in["mlp_b1"],
        "L0_conv_mlp_w2": _L0_conv_in["mlp_w2"],
        "L0_conv_mlp_b2": _L0_conv_in["mlp_b2"],
    }

def reference(x, L0_conv_ln1_w, L0_conv_ln1_b, L0_conv_qkv_w, L0_conv_qkv_b, L0_conv_proj_w, L0_conv_proj_b, L0_conv_ln2_w, L0_conv_ln2_b, L0_conv_mlp_w1, L0_conv_mlp_b1, L0_conv_mlp_w2, L0_conv_mlp_b2):
    import jax
    import jax.numpy as jnp
    def _L0_conv_ref(x, ln1_w, ln1_b, qkv_w, qkv_b, proj_w, proj_b, ln2_w, ln2_b, mlp_w1, mlp_b1, mlp_w2, mlp_b2):
        import jax, jax.numpy as jnp
        import numpy as np
        WS = 7
        SHIFT = 3
        NH = 6

        def layernorm(x, w, b, eps=1e-05):
            mu = jnp.mean(x, axis=-1, keepdims=True)
            var = jnp.var(x, axis=-1, keepdims=True)
            return (x - mu) * jax.lax.rsqrt(var + eps) * w + b
        B, H, W, C = x.shape
        hd = C // NH
        scale = hd ** (-0.5)
        N = WS * WS
        shortcut = x
        xn = layernorm(x, ln1_w, ln1_b)
        xs = jnp.roll(xn, shift=(-SHIFT, -SHIFT), axis=(1, 2))
        xw = xs.reshape(B, H // WS, WS, W // WS, WS, C)
        xw = xw.transpose(0, 1, 3, 2, 4, 5).reshape(-1, N, C)
        qkv = xw @ qkv_w + qkv_b
        qkv = qkv.reshape(-1, N, 3, NH, hd).transpose(2, 0, 3, 1, 4)
        q, k, v = (qkv[0], qkv[1], qkv[2])
        attn = jnp.einsum('bhqd,bhkd->bhqk', q, k) * scale
        attn = jax.nn.softmax(attn, axis=-1)
        o = jnp.einsum('bhqk,bhkd->bhqd', attn, v)
        o = o.transpose(0, 2, 1, 3).reshape(-1, N, C)
        o = o @ proj_w + proj_b
        o = o.reshape(B, H // WS, W // WS, WS, WS, C)
        o = o.transpose(0, 1, 3, 2, 4, 5).reshape(B, H, W, C)
        o = jnp.roll(o, shift=(SHIFT, SHIFT), axis=(1, 2))
        x = shortcut + o
        h = layernorm(x, ln2_w, ln2_b)
        h = jax.nn.gelu(h @ mlp_w1 + mlp_b1, approximate=False)
        x = x + (h @ mlp_w2 + mlp_b2)
        return x

    def _gn(v, G=32, eps=1e-5):
        B_, H_, W_, C_ = v.shape
        g = v.reshape(B_, H_, W_, G, C_ // G)
        m = jnp.mean(g, axis=(1, 2, 4), keepdims=True)
        s = jnp.var(g, axis=(1, 2, 4), keepdims=True)
        return ((g - m) / jnp.sqrt(s + eps)).reshape(v.shape)

    def _ln_c(v, eps=1e-6):
        m = jnp.mean(v, axis=-1, keepdims=True)
        s = jnp.var(v, axis=-1, keepdims=True)
        return (v - m) / jnp.sqrt(s + eps)

    def _ln_t(v, eps=1e-5):
        m = jnp.mean(v, axis=-1, keepdims=True)
        s = jnp.var(v, axis=-1, keepdims=True)
        return (v - m) / jnp.sqrt(s + eps)

    def _to_tokens(v):
        B_, H_, W_, C_ = v.shape
        return v.reshape(B_, H_ * W_, C_)
    def _from_tokens(t, like):
        return t.reshape(like.shape)

    x = _L0_conv_ref(x, L0_conv_ln1_w, L0_conv_ln1_b, L0_conv_qkv_w, L0_conv_qkv_b, L0_conv_proj_w, L0_conv_proj_b, L0_conv_ln2_w, L0_conv_ln2_b, L0_conv_mlp_w1, L0_conv_mlp_b1, L0_conv_mlp_w2, L0_conv_mlp_b2)
    return x


_drawn_inputs = setup_inputs


def setup_inputs(seed=0):
    import zlib

    import numpy as np

    out = dict(_drawn_inputs(seed))
    spreads = {'L0_conv_ln1_w': (1.0, 0.2),
     'L0_conv_ln1_b': (0.0, 0.1),
     'L0_conv_qkv_b': (0.0, 0.1),
     'L0_conv_proj_b': (0.0, 0.1),
     'L0_conv_ln2_w': (1.0, 0.2),
     'L0_conv_ln2_b': (0.0, 0.1),
     'L0_conv_mlp_b1': (0.0, 0.1),
     'L0_conv_mlp_b2': (0.0, 0.1)}
    factors = {}
    for name, (base, spread) in spreads.items():
        noise = np.random.default_rng([zlib.crc32(name.encode()), seed]).standard_normal(out[name].shape)
        drawn = base * np.exp(spread * noise) if base else spread * noise
        out[name] = jnp.asarray(drawn.astype(out[name].dtype))
    for name, factor in factors.items():
        out[name] = (out[name] * factor).astype(out[name].dtype)
    return out
```

```python
from contextlib import ExitStack

import numpy as np

import concourse.bass as bass
from concourse import mybir

ALU = mybir.AluOpType
ACT = mybir.ActivationFunctionType
AX = mybir.AxisListType
F32 = mybir.dt.float32
F32R = mybir.dt.float32r

IMAGES, SIDE, C = 16, 56, 192
WS, SHIFT, HEADS = 7, 3, 6
HD = C // HEADS
TOK = WS * WS
ROWS_W = SIDE // WS
GROUPS = IMAGES * ROWS_W
WIN = ROWS_W
PAIRS = WIN // 2
EVEN = TOK + 1
N = WIN * EVEN
WIDE = 64
COLS = WIN * WIDE
HID = 4 * C
KC = HID // 128
A, B = 128, C - 128
SCALE = float(HD) ** -0.5
EPS = 1e-5
MOVES = 2 * (WIN + 1)


def swin_kernel(nc, x, ln1_w, ln1_b, qkv_w, qkv_b, proj_w, proj_b, ln2_w, ln2_b, mlp_w1, mlp_b1, mlp_w2,
                mlp_b2, out):
    with ExitStack() as ctx:
        def sb(name, shape, dt=F32):
            return ctx.enter_context(nc.sbuf_tensor(name, shape, dt))

        def sem(name):
            return ctx.enter_context(nc.semaphore(name))

        ident = sb("ident", [128, 128])
        raw = sb("raw", [128, 2, HID])
        wqkv = sb("wqkv", [128, 4, 3 * C], F32R)
        wproj = sb("wproj", [128, 4, C], F32R)
        w1 = sb("w1", [128, 4, HID], F32R)
        w2 = sb("w2", [128, 2, KC, C], F32R)
        lnw = sb("lnw", [128, 2, 2])
        lnb = sb("lnb", [128, 2, 2])
        bias = sb("bias", [128, 5 + KC])
        biasf = sb("biasf", [128, 5 + KC])
        projb = sb("projb", [128, C])
        b2 = sb("b2", [128, C])
        mhalf = sb("mhalf", [128, PAIRS])
        eps = sb("eps", [128, PAIRS])
        xin = sb("xin", [128, 2, PAIRS, C])
        xb = sb("xb", [128, PAIRS, C])
        st1 = sb("st1", [128, PAIRS, 6])
        mv1 = sb("mv1", [128, PAIRS, 2])
        ve1 = sb("ve1", [128, PAIRS])
        rs1 = sb("rs1", [128, PAIRS])
        z1 = sb("z1", [128, PAIRS, 256])
        zh1 = sb("zh1", [128, 2, COLS], F32R)
        zl1 = sb("zl1", [128, COLS], F32R)
        qA = sb("qA", [128, N + WIDE - EVEN])
        qB = sb("qB", [64, N + WIDE - EVEN])
        kA = sb("kA", [128, WIN, 4, TOK])
        kB = sb("kB", [64, WIN, 2, TOK])
        vd = sb("vd", [128, PAIRS, 3, 2, 2, HD])
        prob = sb("prob", [128, PAIRS, HEADS, 64])
        mx = sb("mx", [128, PAIRS, HEADS])
        psum_row = sb("psum_row", [128, PAIRS, HEADS])
        rcp = sb("rcp", [128, PAIRS, HEADS])
        pt = sb("pt", [128, PAIRS, 3, 2, TOK])
        oh = sb("oh", [128, 2, COLS], F32R)
        ol = sb("ol", [128, COLS], F32R)
        x2 = sb("x2", [128, PAIRS, C])
        x2b = sb("x2b", [128, PAIRS, C])
        st2 = sb("st2", [128, PAIRS, 6])
        mv2 = sb("mv2", [128, PAIRS, 2])
        ve2 = sb("ve2", [128, PAIRS])
        rs2 = sb("rs2", [128, PAIRS])
        z2 = sb("z2", [128, PAIRS, 256])
        zh2 = sb("zh2", [128, 2, COLS], F32R)
        zl2 = sb("zl2", [128, COLS], F32R)
        g = sb("g", [128, KC, N])
        gh = sb("gh", [128, KC, COLS], F32R)
        gl = sb("gl", [128, KC, COLS], F32R)
        yo = sb("yo", [128, 2, PAIRS, C])

        ps = ctx.enter_context(nc.psum_tensor("ps", [128, 8, 512], F32))
        QK = (0, 5, 6)
        V = 3
        T2 = 1
        S = (7, 0, 5, 6)
        H = (3, 4, 1, 2, 3, 4)
        Y = 1
        T1 = 3
        PV = (7, 0)
        PROJ = 1

        consts_loaded = sem("consts_loaded")
        raw_loaded = sem("raw_loaded")
        ident_ready = sem("ident_ready")
        raw_scaled = sem("raw_scaled")
        w_hi = sem("w_hi")
        w_lo = sem("w_lo")
        bias_mm = sem("bias_mm")
        bias_ready = sem("bias_ready")
        zeroed = sem("zeroed")
        pads_ready = sem("pads_ready")
        x_loaded = [sem("x_loaded0"), sem("x_loaded1")]
        stored = [sem("stored0"), sem("stored1")]
        bn1, mv1_done, ve1_done, rs1_done, z1_done = map(sem, ("bn1", "mv1_done", "ve1_done", "rs1_done", "z1_done"))
        bn2, mv2_done, ve2_done, rs2_done, z2_done = map(sem, ("bn2", "mv2_done", "ve2_done", "rs2_done", "z2_done"))
        xb_done = sem("xb_done")
        x2b_done = sem("x2b_done")
        t1_done, zh1_done, zl1_done = map(sem, ("t1_done", "zh1_done", "zl1_done"))
        t2_done, zh2_done, zl2_done = map(sem, ("t2_done", "zh2_done", "zl2_done"))
        qk_done = sem("qk_done")
        v_done = sem("v_done")
        q_ready = sem("q_ready")
        k_ready = sem("k_ready")
        v_ready = sem("v_ready")
        s_done = sem("s_done")
        smax = sem("smax")
        s_sub = sem("s_sub")
        p_exp = sem("p_exp")
        p_sum = sem("p_sum")
        p_rcp = sem("p_rcp")
        p_norm = sem("p_norm")
        pt_done = sem("pt_done")
        pt_ready = sem("pt_ready")
        pv_done = sem("pv_done")
        oh_ready = sem("oh_ready")
        ol_ready = sem("ol_ready")
        proj_done = sem("proj_done")
        x2_done = sem("x2_done")
        h_done = sem("h_done")
        g_done = sem("g_done")
        gh_ready = sem("gh_ready")
        gl_ready = sem("gl_ready")
        y_done = sem("y_done")
        yo_done = sem("yo_done")

        def wait(eng, s, per_group, group, k):
            v = group * per_group + k
            if not isinstance(v, int) or v > 0:
                eng.wait_ge(s, v)

        def pair_of(buf, pair):
            return buf[:, 2 * WIDE * pair:2 * WIDE * (pair + 1)]

        def windows(cols, n=EVEN, stride=WIDE):
            return cols.rearrange("p (w t) -> p w t", t=stride)[:, :, 0:n]

        def moves(image_rows, win_row):
            top = (image_rows * SIDE + win_row * WS + SHIFT) * SIDE
            low = (image_rows * SIDE + ((win_row + 1) % ROWS_W) * WS) * SIDE
            for w in range(WIN):
                at = 64 * (w % 2)
                for c0, nc_ in (((WS * w + SHIFT, WS),) if w < WIN - 1 else ((WS * w + SHIFT, WS - SHIFT), (0, SHIFT))):
                    for r0, nr in ((top, WS - SHIFT), (low, SHIFT)):
                        yield at, nr * nc_, w // 2, (r0 + c0) * C, [[SIDE * C, nr], [C, nc_], [1, C]]
                        at += nr * nc_

        def iterations(eng, body, last=GROUPS - 2):
            for i in range(3):
                body(i, i % 2)
            with eng.Fori(0, (last - 2) // 2) as j:
                body(j * 2 + 3, 1)
                body(j * 2 + 4, 0)
            for i in range(last + 1, GROUPS + 1):
                body(i, i % 2)

        def attends(i):
            return not isinstance(i, int) or i < GROUPS

        def feeds(i):
            return not isinstance(i, int) or i > 0

        def more(i):
            return not isinstance(i, int) or i < GROUPS - 1

        QKV_ORDER = ((0, 128), (C, C + 128), (A, C), (C + A, 2 * C), (2 * C, 3 * C))
        RAWS = (3 * len(QKV_ORDER), 3, 3, 1)
        NCONST = 12 + 6 + KC + 2

        block = ctx.enter_context(nc.Block())

        @block.sync
        def _(sp):
            nload = 0

            def const(dst, src):
                nonlocal nload
                sp.dma_start(dst, src).then_inc(consts_loaded, 16)
                nload += 1

            def column(v, lo, n):
                return bass.AP(v.tensor, v.offset + lo, [[1, n], [1, 1]])

            def row(v):
                return bass.AP(v.tensor, v.offset, [[0, 128], [1, C]])

            def load_x(g_row, win_row, parity):
                for p0, np_, pair, off, ap in moves(g_row, win_row):
                    sp.dma_start(xin[p0:p0 + np_, parity, pair, :], bass.AP(x.tensor, off, ap))\
                      .then_inc(x_loaded[parity], 16)

            def load_raw(w, segments):
                at = 0
                for lo, hi in segments:
                    cols = slice(at, at + hi - lo)
                    at += hi - lo
                    sp.dma_start(raw[:, 0, cols], w[0:A, lo:hi]).then_inc(raw_loaded, 16)
                    sp.dma_start(raw[0:B, 1, cols], w[A:C, lo:hi]).then_inc(raw_loaded, 16)
                    sp.dma_start(raw[B:128, 1, cols], w[A:C, lo:hi]).then_inc(raw_loaded, 16)

            for n, (w, b) in enumerate(((ln1_w, ln1_b), (ln2_w, ln2_b))):
                for src, dst in ((w, lnw), (b, lnb)):
                    const(dst[:, n, 0:1], column(src, 0, A))
                    const(dst[0:B, n, 1:2], column(src, A, B))
                    const(dst[B:128, n, 1:2], column(src, A, B))
            for t, lo, p0, n in ((0, 0, 0, 128), (1, C, 0, 128), (2, A, 0, 64), (2, C + A, 64, 64),
                                 (3, 2 * C, 0, 128), (4, 2 * C + A, 0, 64)):
                const(bias[p0:p0 + n, t:t + 1], column(qkv_b, lo, n))
            for k in range(KC):
                const(bias[:, 5 + k:6 + k], column(mlp_b1, 128 * k, 128))
            const(projb[:, :], row(proj_b))
            const(b2[:, :], row(mlp_b2))
            assert nload == NCONST
            load_raw(qkv_w, QKV_ORDER)
            sp.wait_ge(zeroed, 1)
            load_x(0, 0, 0)
            sp.wait_ge(w_lo, 1)
            sp.wait_ge(bias_mm, 1)
            load_raw(mlp_w1, ((0, HID),))
            load_x(0, 1, 1)
            sp.wait_ge(w_lo, 2)
            sp.wait_ge(bias_mm, 2)
            load_raw(proj_w, ((0, C),))
            sp.wait_ge(w_lo, 3)
            sp.dma_start(raw[:, :, :].rearrange("p a n -> p (a n)")[:, 0:KC * C]
                         .rearrange("p (k n) -> p k n", n=C),
                         mlp_w2.rearrange("(k p) n -> p k n", p=128)).then_inc(raw_loaded, 16)

            def body(i, parity):
                if not isinstance(i, int) or i < GROUPS - 2:
                    nxt = i + 2
                    wait(sp, z1_done, 1, i, 1)
                    wait(sp, xb_done, 1, i, 1)
                    load_x((nxt // ROWS_W), nxt % ROWS_W, parity)
                if feeds(i):
                    prev = i - 1
                    wait(sp, yo_done, 2, prev, 2)
                    for p0, np_, pair, off, ap in moves(prev // ROWS_W, prev % ROWS_W):
                        sp.dma_start(bass.AP(out.tensor, off, ap), yo[p0:p0 + np_, 1 - parity, pair, :])\
                          .then_inc(stored[1 - parity], 16)

            iterations(sp, body, last=GROUPS - 4)
            sp.wait_ge(stored[0], 16 * MOVES * (GROUPS // 2))
            sp.wait_ge(stored[1], 16 * MOVES * (GROUPS // 2))




        @block.gpsimd
        def _(pool):
            pool.memset(xin[:, :, :, :], 0.0).then_inc(zeroed, 1)
            pool.memset(ident[:, :], 0.0).then_inc(ident_ready, 1)
            pool.wait_ge(ident_ready, 1)
            pool.affine_select(out=ident[:, :], in_=ident[:, :], compare_op=ALU.not_equal, fill=1.0, base=0,
                               pattern=[[-1, 128]], channel_multiplier=1).then_inc(ident_ready, 1)
            pool.memset(mhalf[:, :], -0.5)
            pool.memset(eps[:, :], EPS)
            for t in (kA, kB, vd, prob, x2, x2b, z1, z2):
                pool.memset(t[:], 0.0)
            for t in (zh1, zh2, oh, gh, gl, zl1, zl2, ol, qA, qB):
                last = pool.memset(t[:] if t is qA or t is qB else t[:].bitcast(F32), 0.0)
            last.then_inc(pads_ready, 1)
            pool.wait_ge(pads_ready, 1)
            pool.wait_ge(consts_loaded, 16 * NCONST)

            def add_proj_bias(grp, parity):
                wait(pool, x_loaded[parity], 16 * MOVES, grp // 2, 16 * MOVES)
                wait(pool, x2_done, 2, grp - 1, 2)
                pool.tensor_tensor(xb[:, :, :], xin[:, parity, :, :],
                                   projb[:, :].unsqueeze(1).broadcast_to([128, PAIRS, C]), ALU.add)\
                    .then_inc(xb_done, 1)

            def rstd(mv, ve, rs, mv_done, ve_done, rs_done, grp, used):
                wait(pool, mv_done, 1, grp, 1)
                wait(pool, used, 1, grp - 1, 1)
                pool.tensor_tensor(ve[:, :], mv[:, :, 1], eps[:, :], ALU.add).then_inc(ve_done, 1)
                wait(pool, ve_done, 1, grp, 1)
                pool.tensor_tensor(rs[:, :], ve[:, :], mhalf[:, :], ALU.pow).then_inc(rs_done, 1)

            rstd(mv1, ve1, rs1, mv1_done, ve1_done, rs1_done, 0, z1_done)
            add_proj_bias(0, 0)

            def body(i, parity):
                if feeds(i):
                    prev = i - 1
                    for m in range(KC):
                        wait(pool, gh_ready, KC, prev, m + 1)
                        wait(pool, y_done, 2, prev - 1, 2)
                        pool.tensor_tensor(windows(gl[:, m, :]), windows(g[:, m, :], EVEN, EVEN), windows(gh[:, m, :]).bitcast(F32),
                                           ALU.subtract)\
                            .then_inc(gl_ready, 1)
                if more(i):
                    rstd(mv1, ve1, rs1, mv1_done, ve1_done, rs1_done, i + 1, z1_done)
                if attends(i):
                    wait(pool, p_rcp, 1, i, 1)
                    wait(pool, p_exp, 1, i, 1)
                    pool.tensor_tensor(prob[:, :, :, 0:TOK], prob[:, :, :, 0:TOK],
                                       rcp[:, :, :].unsqueeze(3).broadcast_to([128, PAIRS, HEADS, TOK]), ALU.mult)\
                        .then_inc(p_norm, 1)
                    rstd(mv2, ve2, rs2, mv2_done, ve2_done, rs2_done, i, z2_done)
                    wait(pool, x2_done, 2, i, 2)
                    wait(pool, yo_done, 2, i - 1, 2)
                    pool.tensor_tensor(x2b[:, :, :], x2[:, :, :],
                                       b2[:, :].unsqueeze(1).broadcast_to([128, PAIRS, C]), ALU.add)\
                        .then_inc(x2b_done, 1)
                if more(i):
                    add_proj_bias(i + 1, 1 - parity)

            iterations(pool, body)

        @block.vector
        def _(dve):
            dve.wait_ge(pads_ready, 1)

            def norm_stats(src, st, mv, bn, mv_done, grp):
                for p in range(PAIRS):
                    last = dve.bn_stats(st[:, p, :], src[:, p, :])
                last.then_inc(bn, 1)
                wait(dve, bn, 1, grp, 1)
                dve.nop(nofuse=True)
                for p in range(PAIRS):
                    last = dve.bn_aggr(mv[:, p, :], st[:, p, :])
                last.then_inc(mv_done, 1)

            def norm_apply(src, mv, rs, z, grp, mv_done, rs_done, z_done):
                wait(dve, rs_done, 1, grp, 1)
                wait(dve, mv_done, 1, grp, 1)
                for p in range(PAIRS):
                    dve.tensor_scalar(z[:, p, 0:C], src[:, p, :], mv[:, p, 0:1], rs[:, p:p + 1],
                                      ALU.subtract, ALU.mult)
                    last = dve.tensor_scalar(z[:, p, C:256], src[:, p, A:C], mv[:, p, 0:1], rs[:, p:p + 1],
                                             ALU.subtract, ALU.mult)
                last.then_inc(z_done, 1)

            def low_parts(bank, zh, zl, hi_done, lo_done, grp):
                wait(dve, hi_done, 1, grp, 1)
                dve.tensor_tensor(windows(zl[:, :]), windows(ps[:, bank, :]), windows(zh[:, 0, :]).bitcast(F32),
                                  ALU.subtract)
                dve.tensor_tensor(windows(zh[64:128, 1, :]), windows(ps[64:128, bank + 1, :]),
                                  windows(zh[64:128, 1, :]).bitcast(F32), ALU.subtract).then_inc(lo_done, 1)

            def stats1(grp, parity):
                wait(dve, x_loaded[parity], 16 * MOVES, grp // 2, 16 * MOVES)
                wait(dve, z1_done, 1, grp - 1, 1)
                norm_stats(xin[:, parity, :, :], st1, mv1, bn1, mv1_done, grp)

            def apply1(grp, parity):
                wait(dve, t1_done, 1, grp - 1, 1)
                norm_apply(xin[:, parity, :, :], mv1, rs1, z1, grp, mv1_done, rs1_done, z1_done)

            dve.wait_ge(consts_loaded, 16 * NCONST)
            stats1(0, 0)
            apply1(0, 0)
            for stage, (w, cols, n) in enumerate(((wqkv, 3 * C, 0), (w1, HID, 1), (wproj, C, None))):
                dve.wait_ge(raw_loaded, 16 * sum(RAWS[:stage + 1]))
                if n is not None:
                    dve.wait_ge(bias_mm, stage + 1)
                    for part in range(2):
                        last = dve.tensor_scalar(raw[:, part, 0:cols], raw[:, part, 0:cols], lnw[:, n, part:part + 1],
                                                 None, ALU.mult)
                    last.then_inc(raw_scaled, 1)
                    dve.wait_ge(raw_scaled, stage + 1)
                for part in range(2):
                    last = dve.tensor_copy(w[:, 2 * part, :], raw[:, part, 0:cols])
                last.then_inc(w_hi, 1)
                dve.wait_ge(w_hi, stage + 1)
                for part in range(2):
                    last = dve.tensor_tensor(w[:, 2 * part + 1, :], raw[:, part, 0:cols],
                                             w[:, 2 * part, :].bitcast(F32), ALU.subtract)
                last.then_inc(w_lo, 1)
                if n == 0:
                    dve.tensor_tensor(biasf[:, 0:4], ps[:, 0, 0:4], bias[:, 0:4], ALU.add)
                    dve.tensor_tensor(biasf[0:64, 4:5], ps[0:64, 0, 4:5], bias[0:64, 4:5], ALU.add)\
                       .then_inc(bias_ready, 1)
                if n == 1:
                    dve.tensor_tensor(biasf[:, 5:5 + KC], ps[:, 1, 0:KC], bias[:, 5:5 + KC], ALU.add)\
                       .then_inc(bias_ready, 1)
            dve.wait_ge(raw_loaded, 16 * sum(RAWS))
            raw2 = raw[:, :, :].rearrange("p a n -> p (a n)")[:, 0:KC * C].rearrange("p (k n) -> p k n", n=C)
            dve.tensor_copy(w2[:, 0, :, :], raw2).then_inc(w_hi, 1)
            dve.wait_ge(w_hi, 4)
            dve.tensor_tensor(w2[:, 1, :, :], raw2, w2[:, 0, :, :].bitcast(F32), ALU.subtract).then_inc(w_lo, 1)
            dve.wait_ge(bias_ready, 2)
            low_parts(T1, zh1, zl1, zh1_done, zl1_done, 0)

            def keys(i):
                wait(dve, s_done, PAIRS, i - 1, PAIRS)
                wait(dve, qk_done, 3, i, 2)
                for h in range(4):
                    r = slice(32 * h, 32 * h + 32)
                    last = dve.tensor_scalar(kA[r, :, h, :], windows(ps[r, QK[1], 0:N], TOK, EVEN), biasf[r, 1:2], None, ALU.add)
                last.then_inc(k_ready, 1)
                wait(dve, qk_done, 3, i, 3)
                for h in range(2):
                    r, s = slice(32 * h, 32 * h + 32), slice(64 + 32 * h, 96 + 32 * h)
                    last = dve.tensor_scalar(kB[r, :, h, :], windows(ps[s, QK[2], 0:N], TOK, EVEN), biasf[s, 2:3], None, ALU.add)
                last.then_inc(k_ready, 1)

            def values(i):
                wait(dve, v_done, 1, i, 1)
                wait(dve, pv_done, 1, i - 1, 1)
                vps = ps[:, V:V + 2, :].rearrange("p b (q n) -> p (b q) n", n=256)
                for w in range(2):
                    for par in range(2):
                        src = vps[64 * w:64 * w + 64, :, 0:C].rearrange("p q (j e d) -> p q j e d", j=3, e=2)
                        last = dve.tensor_copy(vd[64 * par:64 * par + 64, :, :, w, par, :], src[:, :, :, par, :])
                last.then_inc(v_ready, 1)

            def scores(i):
                wait(dve, pt_done, PAIRS, i - 1, PAIRS)
                for p in range(PAIRS):
                    s = ps[:, S[p], 0:HEADS * TOK].rearrange("p (h k) -> p h k", k=TOK)
                    wait(dve, s_done, PAIRS, i, p + 1)
                    dve.tensor_reduce(mx[:, p, :], s, AX.X, ALU.max).then_inc(smax, 1)
                    wait(dve, smax, PAIRS, i, p + 1)
                    dve.tensor_tensor(prob[:, p, :, 0:TOK], s,
                                      mx[:, p, :].unsqueeze(2).broadcast_to([128, HEADS, TOK]), ALU.subtract)\
                       .then_inc(s_sub, 1)

            def hidden_hi(prev):
                for m in range(KC):
                    wait(dve, g_done, KC, prev, m + 1)
                    wait(dve, y_done, 2, prev - 1, 2)
                    dve.tensor_copy(windows(gh[:, m, :]), windows(g[:, m, :], EVEN, EVEN)).then_inc(gh_ready, 1)

            def residual(i, half, bank, src, dst, add_done):
                dve.tensor_tensor(dst[:, 2 * half:2 * half + 2, :],
                                  ps[:, bank + half, :].rearrange("p (q n) -> p q n", n=256)[:, :, 0:C],
                                  src[:, 2 * half:2 * half + 2, :], ALU.add).then_inc(add_done, 1)

            def body(i, parity):
                prev = i - 1
                if attends(i):
                    keys(i)
                    values(i)
                if feeds(i):
                    low_parts(T2, zh2, zl2, zh2_done, zl2_done, prev)
                if attends(i):
                    scores(i)
                if more(i):
                    stats1(i + 1, 1 - parity)
                if feeds(i):
                    hidden_hi(prev)
                if more(i):
                    apply1(i + 1, 1 - parity)
                if attends(i):
                    wait(dve, p_exp, 1, i, 1)
                    dve.tensor_reduce(psum_row[:, :, :], prob[:, :, :, 0:TOK], AX.X, ALU.add).then_inc(p_sum, 1)
                    wait(dve, p_sum, 1, i, 1)
                    dve.reciprocal(rcp[:, :, :], psum_row[:, :, :]).then_inc(p_rcp, 1)
                if feeds(i):
                    wait(dve, x2b_done, 1, prev, 1)
                    wait(dve, stored[1 - parity], 16 * MOVES, prev // 2, 0)
                    for half in range(2):
                        wait(dve, y_done, 2, prev, half + 1)
                        residual(prev, half, Y, x2b, yo[:, 1 - parity, :, :], yo_done)
                if more(i):
                    low_parts(T1, zh1, zl1, zh1_done, zl1_done, i + 1)
                if attends(i):
                    wait(dve, oh_ready, 1, i, 1)
                    dve.scalar_tensor_tensor(windows(ol[:, :], TOK), windows(ps[:, PV[0], 0:N], TOK, EVEN),
                                             biasf[:, 3:4], windows(oh[:, 0, :], TOK).bitcast(F32),
                                             ALU.add, ALU.subtract)
                    dve.scalar_tensor_tensor(windows(oh[64:128, 1, :], TOK), windows(ps[0:64, PV[1], 0:N], TOK, EVEN),
                                             biasf[0:64, 4:5], windows(oh[0:64, 1, :], TOK).bitcast(F32), ALU.add, ALU.subtract)\
                       .then_inc(ol_ready, 1)
                    wait(dve, xb_done, 1, i, 1)
                    wait(dve, x2b_done, 1, i - 1, 1)
                    wait(dve, z2_done, 1, i - 1, 1)
                    for half in range(2):
                        wait(dve, proj_done, 2, i, half + 1)
                        residual(i, half, PROJ, xb, x2, x2_done)
                    wait(dve, x2_done, 2, i, 2)
                    norm_stats(x2, st2, mv2, bn2, mv2_done, i)
                    wait(dve, t2_done, 1, i - 1, 1)
                    norm_apply(x2, mv2, rs2, z2, i, mv2_done, rs2_done, z2_done)

            iterations(dve, body)

        @block.scalar
        def _(act):
            act.wait_ge(pads_ready, 1)
            act.wait_ge(bias_ready, 2)

            def high_parts(bank, zh, t_done, hi_done, grp):
                wait(act, t_done, 1, grp, 1)
                act.activation(zh[:, :, :].rearrange("p a (w t) -> p a w t", t=WIDE)[:, :, :, 0:EVEN],
                               ps[:, bank:bank + 2, :].rearrange("p a (w t) -> p a w t", t=WIDE)[:, :, :, 0:EVEN],
                               ACT.Copy).then_inc(hi_done, 1)

            high_parts(T1, zh1, t1_done, zh1_done, 0)

            def body(i, parity):
                prev = i - 1
                if attends(i):
                    wait(act, s_done, PAIRS, i - 1, PAIRS)
                    wait(act, qk_done, 3, i, 1)
                    act.activation(qA[:, 0:N], ps[:, QK[0], 0:N], ACT.Identity, bias=biasf[:, 0:1]).then_inc(q_ready, 1)
                    wait(act, qk_done, 3, i, 3)
                    act.activation(qB[:, 0:N], ps[0:64, QK[2], 0:N], ACT.Identity, bias=biasf[0:64, 2:3])\
                       .then_inc(q_ready, 1)
                if feeds(i):
                    wait(act, h_done, KC, prev - 1, KC)
                    high_parts(T2, zh2, t2_done, zh2_done, prev)
                    for m in range(KC):
                        wait(act, h_done, KC, prev, m + 1)
                        wait(act, gl_ready, KC, prev - 1, m + 1)
                        act.activation(g[:, m, :], ps[:, H[m], 0:N], ACT.Gelu, bias=biasf[:, 5 + m:6 + m])\
                           .then_inc(g_done, 1)
                if attends(i):
                    wait(act, s_sub, PAIRS, i, PAIRS)
                    act.activation(prob[:, :, :, 0:TOK], prob[:, :, :, 0:TOK], ACT.Exp, scale=SCALE).then_inc(p_exp, 1)
                    wait(act, pv_done, 1, i - 1, 1)
                    for p in range(PAIRS):
                        wait(act, pt_done, PAIRS, i, p + 1)
                        act.activation(pt[:, p, :, :, :],
                                       ps[:, S[p], 0:384].rearrange("p (j w q) -> p j w q", j=3, w=2)[:, :, :, 0:TOK],
                                       ACT.Copy).then_inc(pt_ready, 1)
                if more(i):
                    wait(act, v_done, 1, i, 1)
                    high_parts(T1, zh1, t1_done, zh1_done, i + 1)
                if attends(i):
                    wait(act, pv_done, 1, i, 1)
                    wait(act, proj_done, 2, i - 1, 2)
                    act.activation(windows(oh[:, 0, :], TOK), windows(ps[:, PV[0], 0:N], TOK, EVEN), ACT.Identity,
                                   bias=biasf[:, 3:4])
                    act.activation(windows(oh[0:64, 1, :], TOK), windows(ps[0:64, PV[1], 0:N], TOK, EVEN), ACT.Identity,
                                   bias=biasf[0:64, 4:5])\
                       .then_inc(oh_ready, 1)

            iterations(act, body)

        @block.tensor
        def _(pe):
            pe.wait_ge(pads_ready, 1)
            pe.wait_ge(ident_ready, 2)
            pe.wait_ge(consts_loaded, 16 * NCONST)

            def transposes(bank, z, t_done):
                for p in range(PAIRS):
                    for part in range(2):
                        last = pe.transpose(ps[:, bank + part, 128 * p:128 * p + 128],
                                            z[:, p, 128 * part:128 * part + 128], ident[:, :])
                last.then_inc(t_done, 1)

            def offsets(bank, n, tiles):
                for col, (c0, m) in enumerate(tiles):
                    pe.matmul(ps[0:m, bank, col:col + 1], raw[:, 0, c0:c0 + m], lnb[:, n, 0:1], start=True, stop=False)
                    last = pe.matmul(ps[0:m, bank, col:col + 1], raw[0:64, 1, c0:c0 + m], lnb[0:64, n, 1:2],
                                     start=False, stop=True)
                last.then_inc(bias_mm, 1)

            pe.wait_ge(raw_loaded, 16 * RAWS[0])
            offsets(0, 0, [(128 * t, 128) for t in range(4)] + [(512, 64)])
            wait(pe, z1_done, 1, 0, 1)
            transposes(T1, z1, t1_done)
            pe.wait_ge(raw_loaded, 16 * (RAWS[0] + RAWS[1]))
            offsets(1, 1, [(128 * k, 128) for k in range(KC)])
            pe.wait_ge(w_lo, 4)
            pe.wait_ge(bias_ready, 2)

            def project(dst, zh, zl, w, cols, pair=None):
                for n, (act_, part) in enumerate(((zh[:, 0, :], 0), (zh[:, 0, :], 1), (zl[:, :], 0),
                                                  (zh[:, 1, :], 2), (zh[:, 1, :], 3))):
                    if pair is None:
                        last = pe.matmul(dst, cols(w, part), windows(act_), start=(n == 0), stop=(n == 4))
                    else:
                        last = pe.matmul(dst, pair_of(act_, pair), cols(w, part), start=(n == 0), stop=(n == 4))
                return last

            def qk(i):
                wait(pe, zh1_done, 1, i, 1)
                wait(pe, zl1_done, 1, i, 1)
                wait(pe, ol_ready, 1, i - 1, 1)
                for t in range(3):
                    project(ps[:, QK[t], 0:N], zh1, zl1, wqkv, lambda w, part: w[:, part, 128 * t:128 * t + 128])\
                        .then_inc(qk_done, 1)

            def v(i):
                for p in range(PAIRS):
                    last = project(ps[:, V + p // 2, 256 * (p % 2):256 * (p % 2) + C], zh1, zl1, wqkv,
                                   lambda w, part: w[:, part, 2 * C:3 * C], pair=p)
                last.then_inc(v_done, 1)

            def s(i):
                wait(pe, q_ready, 2, i, 2)
                wait(pe, k_ready, 2, i, 2)
                for p in range(PAIRS):
                    for w in range(2):
                        c0, r = (2 * p + w) * EVEN, slice(64 * w, 64 * w + 64)
                        pe.matmul(ps[r, S[p], 0:4 * TOK], qA[:, c0:c0 + WIDE],
                                  kA[:, 2 * p + w, :, :].rearrange("p h k -> p (h k)"), start=True, stop=True)
                        last = pe.matmul(ps[r, S[p], 4 * TOK:6 * TOK], qB[:, c0:c0 + WIDE],
                                         kB[:, 2 * p + w, :, :].rearrange("p h k -> p (h k)"), start=True, stop=True)
                    last.then_inc(s_done, 1)

            def mlp1(prev):
                wait(pe, zh2_done, 1, prev, 1)
                wait(pe, zl2_done, 1, prev, 1)
                for m in range(KC):
                    if m < 2:
                        if m == 0:
                            wait(pe, v_ready, 1, prev + 1, 1) if attends(prev + 1) else None
                    elif m >= 4:
                        wait(pe, g_done, KC, prev, m - 3)
                    project(ps[:, H[m], 0:N], zh2, zl2, w1, lambda w, part: w[:, part, 128 * m:128 * m + 128])\
                        .then_inc(h_done, 1)

            def mlp2(prev, pairs):
                if 0 in pairs:
                    wait(pe, g_done, KC, prev, 4)
                for p in pairs:
                    for k in range(KC):
                        if p == 0:
                            wait(pe, gh_ready, KC, prev, k + 1)
                        dst = ps[:, Y + p // 2, 256 * (p % 2):256 * (p % 2) + C]
                        pe.matmul(dst, pair_of(gh[:, k, :], p), w2[:, 0, k, :], start=(k == 0), stop=False)
                        pe.matmul(dst, pair_of(gh[:, k, :], p), w2[:, 1, k, :], start=False, stop=False)
                        if p == 0:
                            wait(pe, gl_ready, KC, prev, k + 1)
                        last = pe.matmul(dst, pair_of(gl[:, k, :], p), w2[:, 0, k, :], start=False, stop=(k == KC - 1))
                    if p % 2:
                        last.then_inc(y_done, 1)

            def turn_probs(i):
                wait(pe, p_norm, 1, i, 1)
                for p in range(PAIRS):
                    for j in range(3):
                        last = pe.transpose(ps[:, S[p], 128 * j:128 * j + 128],
                                            prob[:, p, 2 * j:2 * j + 2, :].rearrange("p h k -> p (h k)"), ident[:, :])
                    last.then_inc(pt_done, 1)

            def pv(i):
                wait(pe, v_ready, 1, i, 1)
                wait(pe, pt_ready, PAIRS, i, PAIRS)
                for p in range(PAIRS):
                    for w in range(2):
                        c0 = (2 * p + w) * EVEN
                        for j in range(3):
                            r = slice(64 * (j % 2), 64 * (j % 2) + 64)
                            last = pe.matmul(ps[r, PV[j // 2], c0:c0 + TOK],
                                             vd[:, p, j, w, :, :].rearrange("p e d -> p (e d)"),
                                             pt[:, p, j, w, :], start=True, stop=True)
                last.then_inc(pv_done, 1)

            def proj(i):
                wait(pe, oh_ready, 1, i, 1)
                wait(pe, ol_ready, 1, i, 1)
                wait(pe, yo_done, 2, i - 1, 2)
                for p in range(PAIRS):
                    last = project(ps[:, PROJ + p // 2, 256 * (p % 2):256 * (p % 2) + C], oh, ol, wproj,
                                   lambda w, part: w[:, part, :], pair=p)
                    if p % 2:
                        last.then_inc(proj_done, 1)

            def body(i, parity):
                prev = i - 1
                if attends(i):
                    qk(i)
                    v(i)
                if feeds(i):
                    wait(pe, z2_done, 1, prev, 1)
                    wait(pe, x2_done, 2, prev, 2)
                    transposes(T2, z2, t2_done)
                if attends(i):
                    s(i)
                if feeds(i):
                    mlp1(prev)
                    mlp2(prev, (0, 1))
                if attends(i):
                    turn_probs(i)
                if feeds(i):
                    mlp2(prev, (2,))
                if more(i):
                    wait(pe, z1_done, 1, i + 1, 1)
                    if feeds(i):
                        wait(pe, g_done, KC, prev, KC)
                    transposes(T1, z1, t1_done)
                if feeds(i):
                    mlp2(prev, (3,))
                if attends(i):
                    pv(i)
                    proj(i)

            iterations(pe, body)


_INS = ["x"] + ["L0_conv_" + n for n in ("ln1_w", "ln1_b", "qkv_w", "qkv_b", "proj_w", "proj_b", "ln2_w", "ln2_b",
                                         "mlp_w1", "mlp_b1", "mlp_w2", "mlp_b2")]


def kernel(**inputs):
    import concourse.bacc as bacc
    from concourse.bass_utils import run_bass_kernel_spmd

    nc = bacc.Bacc("TRN2", target_bir_lowering=False, num_devices=1)
    arrays, args = {}, []
    for name in _INS:
        a = np.ascontiguousarray(inputs[name])
        arrays[f"in_{name}"] = a
        args.append(nc.dram_tensor(f"in_{name}", a.shape, mybir.dt.from_np(a.dtype), kind="ExternalInput").ap())
    out = nc.dram_tensor("out", (IMAGES, SIDE, SIDE, C), F32, kind="ExternalOutput").ap()
    swin_kernel(nc, *args, out)
    r = run_bass_kernel_spmd(nc, [arrays], core_ids=[0])
    return r.results[0]["out"]
```

```python
from contextlib import ExitStack

import numpy as np

import concourse.bass as bass
from concourse import mybir

ALU = mybir.AluOpType
ACT = mybir.ActivationFunctionType
AX = mybir.AxisListType
F32 = mybir.dt.float32
F32R = mybir.dt.float32r

IMAGES, SIDE, C = 16, 56, 192
WS, SHIFT, HEADS = 7, 3, 6
HD = C // HEADS
TOK = WS * WS
ROWS_W = SIDE // WS
GROUPS = IMAGES * ROWS_W
WIN = ROWS_W
PAIRS = WIN // 2
EVEN = TOK + 1
N = WIN * EVEN
WIDE = 64
M = WIN * TOK
COLS = WIN * WIDE
HID = 4 * C
KC = HID // 128
A, B = 128, C - 128
SCALE = float(HD) ** -0.5
EPS = 1e-5
MOVES = 2 * (WIN + 1)


def swin_kernel(nc, x, ln1_w, ln1_b, qkv_w, qkv_b, proj_w, proj_b, ln2_w, ln2_b, mlp_w1, mlp_b1, mlp_w2,
                mlp_b2, out):
    with ExitStack() as ctx:
        def sb(name, shape, dt=F32):
            return ctx.enter_context(nc.sbuf_tensor(name, shape, dt))

        def sem(name):
            return ctx.enter_context(nc.semaphore(name))

        ident = sb("ident", [128, 128])
        raw = sb("raw", [128, 2, HID])
        wqkv = sb("wqkv", [128, 4, 3 * C], F32R)
        wproj = sb("wproj", [128, 4, C], F32R)
        w1 = sb("w1", [128, 4, HID], F32R)
        w2 = sb("w2", [128, KC, 4, 128], F32R)
        lnw = sb("lnw", [128, 2, 2])
        lnb = sb("lnb", [128, 2, 2])
        bias = sb("bias", [128, 5 + KC])
        biasf = sb("biasf", [128, 5 + KC])
        projb = sb("projb", [128, C])
        b2 = sb("b2", [128, 2])
        twice = sb("twice", [128, B])
        mhalf = sb("mhalf", [128, PAIRS])
        eps = sb("eps", [128, PAIRS])
        xin = sb("xin", [128, 2, PAIRS, C])
        xb = sb("xb", [128, PAIRS, C])
        st1 = sb("st1", [128, PAIRS, 6])
        mv1 = sb("mv1", [128, PAIRS, 2])
        ve1 = sb("ve1", [128, PAIRS])
        rs1 = sb("rs1", [128, PAIRS])
        z1 = sb("z1", [128, PAIRS, C])
        zh1 = sb("zh1", [128, 2, COLS], F32R)
        zl1 = sb("zl1", [128, COLS], F32R)
        qA = sb("qA", [128, N + WIDE - EVEN])
        qB = sb("qB", [64, N + WIDE - EVEN])
        kA = sb("kA", [128, WIN, 4, TOK])
        kB = sb("kB", [64, WIN, 2, TOK])
        vd = sb("vd", [128, PAIRS, 3, 2, 2, HD])
        prob = sb("prob", [128, PAIRS, HEADS, 64])
        mx = sb("mx", [128, PAIRS, HEADS])
        psum_row = sb("psum_row", [128, PAIRS, HEADS])
        rcp = sb("rcp", [128, PAIRS, HEADS])
        pt = sb("pt", [128, PAIRS, 3, 2, TOK])
        oh = sb("oh", [128, 2, COLS], F32R)
        ol = sb("ol", [128, COLS], F32R)
        x2 = sb("x2", [128, PAIRS, C])
        st2 = sb("st2", [128, PAIRS, 6])
        mv2 = sb("mv2", [128, PAIRS, 2])
        ve2 = sb("ve2", [128, PAIRS])
        rs2 = sb("rs2", [128, PAIRS])
        z2 = sb("z2", [128, PAIRS, C])
        zh2 = sb("zh2", [128, 2, M], F32R)
        zl2 = sb("zl2", [128, M], F32R)
        g = sb("g", [128, KC, M])
        gh = sb("gh", [128, KC, M], F32R)
        gl = sb("gl", [128, KC, M], F32R)
        yT = sb("yT", [128, 2, COLS])
        yo = sb("yo", [128, 2, PAIRS, C])
        spare = sb("spare", [1, 1])

        ps = ctx.enter_context(nc.psum_tensor("ps", [128, 8, 512], F32))
        QK = (0, 1, 6)
        V = 3
        S = (5, 2, 0, 1)
        T2 = 6
        H = (5, 2, 7, 6, 3, 4)
        Y = (5, 2)
        TY = (5, 2)
        T1 = 3
        TP = (0, 1, 7, 6)
        PV = (0, 1)
        PROJ = (3, 7)

        consts_loaded = sem("consts_loaded")
        raw_loaded = sem("raw_loaded")
        ident_ready = sem("ident_ready")
        twice_ready = sem("twice_ready")
        raw_scaled = sem("raw_scaled")
        w_hi = sem("w_hi")
        w_lo = sem("w_lo")
        bias_mm = sem("bias_mm")
        bias_ready = sem("bias_ready")
        zeroed = sem("zeroed")
        pads_ready = sem("pads_ready")
        x_loaded = [sem("x_loaded0"), sem("x_loaded1")]
        stored = [sem("stored0"), sem("stored1")]
        bn1, mv1_done, ve1_done, rs1_done, z1_done = map(sem, ("bn1", "mv1_done", "ve1_done", "rs1_done", "z1_done"))
        bn2, mv2_done, ve2_done, rs2_done, z2_done = map(sem, ("bn2", "mv2_done", "ve2_done", "rs2_done", "z2_done"))
        xb_done = sem("xb_done")
        t1_done, zh1_done, zl1_done = map(sem, ("t1_done", "zh1_done", "zl1_done"))
        t2_done, zh2_done, zl2_done = map(sem, ("t2_done", "zh2_done", "zl2_done"))
        qk_done = sem("qk_done")
        v_done = sem("v_done")
        qk_ready = sem("qk_ready")
        v_ready = sem("v_ready")
        s_done = sem("s_done")
        smax = sem("smax")
        s_sub = sem("s_sub")
        p_exp = sem("p_exp")
        p_sum = sem("p_sum")
        p_rcp = sem("p_rcp")
        p_norm = sem("p_norm")
        pt_done = sem("pt_done")
        pt_ready = sem("pt_ready")
        pv_done = sem("pv_done")
        spare_done = sem("spare_done")
        oh_ready = sem("oh_ready")
        ol_ready = sem("ol_ready")
        proj_done = sem("proj_done")
        x2_done = sem("x2_done")
        h_done = sem("h_done")
        g_done = sem("g_done")
        gh_ready = sem("gh_ready")
        gl_ready = sem("gl_ready")
        y_done = sem("y_done")
        yT_ready = sem("yT_ready")
        ty_done = sem("ty_done")
        yo_done = sem("yo_done")

        def wait(eng, s, per_group, group, k):
            v = group * per_group + k
            if not isinstance(v, int) or v > 0:
                eng.wait_ge(s, v)

        def pair_of(buf, pair):
            return buf[:, 2 * WIDE * pair:2 * WIDE * (pair + 1)]

        def windows(cols, n=EVEN, stride=WIDE):
            return cols.rearrange("p (w t) -> p w t", t=stride)[:, :, 0:n]

        def moves(image_rows, win_row):
            top = (image_rows * SIDE + win_row * WS + SHIFT) * SIDE
            low = (image_rows * SIDE + ((win_row + 1) % ROWS_W) * WS) * SIDE
            for w in range(WIN):
                at = 64 * (w % 2)
                for c0, nc_ in (((WS * w + SHIFT, WS),) if w < WIN - 1 else ((WS * w + SHIFT, WS - SHIFT), (0, SHIFT))):
                    for r0, nr in ((top, WS - SHIFT), (low, SHIFT)):
                        yield at, nr * nc_, w // 2, (r0 + c0) * C, [[SIDE * C, nr], [C, nc_], [1, C]]
                        at += nr * nc_

        def iterations(eng, body, last=GROUPS - 4):
            for i in range(3):
                body(i, i % 2)
            with eng.Fori(0, (last - 2) // 2) as j:
                body(j * 2 + 3, 1)
                body(j * 2 + 4, 0)
            for i in range(last + 1, GROUPS + 1):
                body(i, i % 2)

        def attends(i):
            return not isinstance(i, int) or i < GROUPS

        def feeds(i):
            return not isinstance(i, int) or i > 0

        def more(i):
            return not isinstance(i, int) or i < GROUPS - 1

        QKV_ORDER = ((0, 128), (C, C + 128), (A, C), (C + A, 2 * C), (2 * C, 3 * C))
        RAWS = (3 * len(QKV_ORDER), 3, 3, 1)
        NCONST = 12 + 6 + KC + 3

        block = ctx.enter_context(nc.Block())

        @block.sync
        def _(sp):
            nload = 0

            def const(dst, src):
                nonlocal nload
                sp.dma_start(dst, src).then_inc(consts_loaded, 16)
                nload += 1

            def column(v, lo, n):
                return bass.AP(v.tensor, v.offset + lo, [[1, n], [1, 1]])

            def row(v):
                return bass.AP(v.tensor, v.offset, [[0, 128], [1, C]])

            def load_x(g_row, win_row, parity):
                for p0, np_, pair, off, ap in moves(g_row, win_row):
                    sp.dma_start(xin[p0:p0 + np_, parity, pair, :], bass.AP(x.tensor, off, ap))\
                      .then_inc(x_loaded[parity], 16)

            def load_raw(w, segments):
                at = 0
                for lo, hi in segments:
                    cols = slice(at, at + hi - lo)
                    at += hi - lo
                    sp.dma_start(raw[:, 0, cols], w[0:A, lo:hi]).then_inc(raw_loaded, 16)
                    sp.dma_start(raw[0:B, 1, cols], w[A:C, lo:hi]).then_inc(raw_loaded, 16)
                    sp.dma_start(raw[B:128, 1, cols], w[A:C, lo:hi]).then_inc(raw_loaded, 16)

            sp.wait_ge(zeroed, 2)
            for n, (w, b) in enumerate(((ln1_w, ln1_b), (ln2_w, ln2_b))):
                for src, dst in ((w, lnw), (b, lnb)):
                    const(dst[:, n, 0:1], column(src, 0, A))
                    const(dst[0:B, n, 1:2], column(src, A, B))
                    const(dst[B:128, n, 1:2], column(src, A, B))
            for t, lo, p0, n in ((0, 0, 0, 128), (1, C, 0, 128), (2, A, 0, 64), (2, C + A, 64, 64),
                                 (3, 2 * C, 0, 128), (4, 2 * C + A, 0, 64)):
                const(bias[p0:p0 + n, t:t + 1], column(qkv_b, lo, n))
            for k in range(KC):
                const(bias[:, 5 + k:6 + k], column(mlp_b1, 128 * k, 128))
            const(projb[:, :], row(proj_b))
            const(b2[:, 0:1], column(mlp_b2, 0, A))
            const(b2[0:B, 1:2], column(mlp_b2, A, B))
            assert nload == NCONST
            load_raw(qkv_w, QKV_ORDER)
            load_x(0, 0, 0)
            sp.wait_ge(w_lo, 1)
            sp.wait_ge(bias_mm, 1)
            load_raw(mlp_w1, ((0, HID),))
            load_x(0, 1, 1)
            sp.wait_ge(w_lo, 2)
            sp.wait_ge(bias_mm, 2)
            load_raw(proj_w, ((0, C),))
            sp.wait_ge(w_lo, 3)
            sp.dma_start(raw[:, :, :].rearrange("p a n -> p (a n)")[:, 0:KC * C]
                         .rearrange("p (k n) -> p k n", n=C),
                         mlp_w2.rearrange("(k p) n -> p k n", p=128)).then_inc(raw_loaded, 16)

            def body(i, parity):
                if not isinstance(i, int) or i < GROUPS - 2:
                    nxt = i + 2
                    wait(sp, z1_done, 1, i, 1)
                    wait(sp, xb_done, 1, i, 1)
                    load_x((nxt // ROWS_W), nxt % ROWS_W, parity)
                if feeds(i):
                    prev = i - 1
                    wait(sp, yo_done, 2, prev, 2)
                    for p0, np_, pair, off, ap in moves(prev // ROWS_W, prev % ROWS_W):
                        sp.dma_start(bass.AP(out.tensor, off, ap), yo[p0:p0 + np_, 1 - parity, pair, :])\
                          .then_inc(stored[1 - parity], 16)

            iterations(sp, body)
            sp.wait_ge(stored[0], 16 * MOVES * (GROUPS // 2))
            sp.wait_ge(stored[1], 16 * MOVES * (GROUPS // 2))




        @block.gpsimd
        def _(pool):
            pool.memset(b2[:, :], 0.0).then_inc(zeroed, 1)
            pool.memset(xin[:, :, :, :], 0.0).then_inc(zeroed, 1)
            pool.memset(twice[:, :], 0.0).then_inc(twice_ready, 1)
            pool.memset(ident[:, :], 0.0).then_inc(ident_ready, 1)
            for n in range(2):
                pool.wait_ge(twice_ready, n + 1)
                pool.affine_select(out=twice[:, :], in_=twice[:, :], compare_op=ALU.not_equal, fill=1.0, base=-B * n,
                                   pattern=[[-1, B]], channel_multiplier=1).then_inc(twice_ready, 1)
            pool.wait_ge(ident_ready, 1)
            pool.affine_select(out=ident[:, :], in_=ident[:, :], compare_op=ALU.not_equal, fill=1.0, base=0,
                               pattern=[[-1, 128]], channel_multiplier=1).then_inc(ident_ready, 1)
            pool.memset(mhalf[:, :], -0.5)
            pool.memset(eps[:, :], EPS)
            for t in (kA, kB, vd, prob, x2, z1, z2, yT):
                pool.memset(t[:], 0.0)
            for t in (zh1, oh, zl1, ol, w2, qA, qB):
                last = pool.memset(t[:] if t is qA or t is qB else t[:].bitcast(F32), 0.0)
            last.then_inc(pads_ready, 1)
            pool.wait_ge(pads_ready, 1)
            pool.wait_ge(consts_loaded, 16 * NCONST)

            def add_proj_bias(grp, parity):
                wait(pool, x_loaded[parity], 16 * MOVES, grp // 2, 16 * MOVES)
                wait(pool, x2_done, 2, grp - 1, 2)
                pool.tensor_tensor(xb[:, :, :], xin[:, parity, :, :],
                                   projb[:, :].unsqueeze(1).broadcast_to([128, PAIRS, C]), ALU.add)\
                    .then_inc(xb_done, 1)

            def rstd(mv, ve, rs, mv_done, ve_done, rs_done, grp, used):
                wait(pool, mv_done, 1, grp, 1)
                wait(pool, used, 1, grp - 1, 1)
                pool.tensor_tensor(ve[:, :], mv[:, :, 1], eps[:, :], ALU.add).then_inc(ve_done, 1)
                wait(pool, ve_done, 1, grp, 1)
                pool.tensor_tensor(rs[:, :], ve[:, :], mhalf[:, :], ALU.pow).then_inc(rs_done, 1)

            rstd(mv1, ve1, rs1, mv1_done, ve1_done, rs1_done, 0, z1_done)
            add_proj_bias(0, 0)
            rstd(mv1, ve1, rs1, mv1_done, ve1_done, rs1_done, 1, z1_done)

            def body(i, parity):
                prev = i - 1
                if feeds(i):
                    for m in range(KC):
                        wait(pool, gh_ready, KC, prev, m + 1)
                        wait(pool, y_done, 2, prev - 1, 2)
                        pool.tensor_tensor(gl[:, m, :], g[:, m, :], gh[:, m, :].bitcast(F32), ALU.subtract)\
                            .then_inc(gl_ready, 1)
                if attends(i):
                    for p in range(PAIRS):
                        wait(pool, p_rcp, 2, i, p // 2 + 1)
                        pool.tensor_tensor(prob[:, p, :, 0:TOK], prob[:, p, :, 0:TOK],
                                           rcp[:, p, :].unsqueeze(2).broadcast_to([128, HEADS, TOK]), ALU.mult)\
                            .then_inc(p_norm, 1)
                    rstd(mv2, ve2, rs2, mv2_done, ve2_done, rs2_done, i, z2_done)
                    if more(i + 1):
                        rstd(mv1, ve1, rs1, mv1_done, ve1_done, rs1_done, i + 2, z1_done)
                if more(i):
                    add_proj_bias(i + 1, 1 - parity)

            iterations(pool, body)

        @block.vector
        def _(dve):
            dve.wait_ge(pads_ready, 1)

            def norm_stats(src, st, mv, bn, mv_done, grp):
                for p in range(PAIRS):
                    last = dve.bn_stats(st[:, p, :], src[:, p, :])
                last.then_inc(bn, 1)
                wait(dve, bn, 1, grp, 1)
                dve.nop(nofuse=True)
                for p in range(PAIRS):
                    last = dve.bn_aggr(mv[:, p, :], st[:, p, :])
                last.then_inc(mv_done, 1)

            def norm_apply(src, mv, rs, z, grp, mv_done, rs_done, z_done):
                wait(dve, rs_done, 1, grp, 1)
                wait(dve, mv_done, 1, grp, 1)
                for p in range(PAIRS):
                    last = dve.tensor_scalar(z[:, p, :], src[:, p, :], mv[:, p, 0:1], rs[:, p:p + 1],
                                             ALU.subtract, ALU.mult)
                last.then_inc(z_done, 1)

            def low_parts(bank, zh, zl, hi_done, lo_done, grp):
                stride, n = (WIDE, EVEN) if zh is zh1 else (TOK, TOK)
                wait(dve, hi_done, 1, grp, 1)
                dve.tensor_tensor(windows(zl[:, :], n, stride), windows(ps[:, bank, :], n),
                                  windows(zh[:, 0, :], n, stride).bitcast(F32), ALU.subtract)
                dve.tensor_tensor(windows(zh[0:64, 1, :], n, stride), windows(ps[64:128, bank + 1, :], n),
                                  windows(zh[64:128, 1, :], n, stride).bitcast(F32), ALU.subtract).then_inc(lo_done, 1)

            def stats1(grp, parity):
                wait(dve, x_loaded[parity], 16 * MOVES, grp // 2, 16 * MOVES)
                wait(dve, z1_done, 1, grp - 1, 1)
                norm_stats(xin[:, parity, :, :], st1, mv1, bn1, mv1_done, grp)

            def apply1(grp, parity):
                wait(dve, t1_done, 1, grp - 1, 1)
                norm_apply(xin[:, parity, :, :], mv1, rs1, z1, grp, mv1_done, rs1_done, z1_done)

            dve.wait_ge(consts_loaded, 16 * NCONST)
            stats1(0, 0)
            apply1(0, 0)
            for stage, (w, cols, n) in enumerate(((wqkv, 3 * C, 0), (w1, HID, 1), (wproj, C, None))):
                dve.wait_ge(raw_loaded, 16 * sum(RAWS[:stage + 1]))
                if n is not None:
                    dve.wait_ge(bias_mm, stage + 1)
                    for part in range(2):
                        last = dve.tensor_scalar(raw[:, part, 0:cols], raw[:, part, 0:cols], lnw[:, n, part:part + 1],
                                                 None, ALU.mult)
                    last.then_inc(raw_scaled, 1)
                    dve.wait_ge(raw_scaled, stage + 1)
                for part in range(2):
                    last = dve.tensor_copy(w[:, 2 * part, :], raw[:, part, 0:cols])
                last.then_inc(w_hi, 1)
                dve.wait_ge(w_hi, stage + 1)
                for part in range(2):
                    last = dve.tensor_tensor(w[:, 2 * part + 1, :], raw[:, part, 0:cols],
                                             w[:, 2 * part, :].bitcast(F32), ALU.subtract)
                last.then_inc(w_lo, 1)
                if n == 0:
                    dve.tensor_tensor(biasf[:, 0:4], ps[:, 0, 0:4], bias[:, 0:4], ALU.add)
                    dve.tensor_tensor(biasf[0:64, 4:5], ps[0:64, 0, 4:5], bias[0:64, 4:5], ALU.add)\
                       .then_inc(bias_ready, 1)
                if n == 1:
                    dve.tensor_tensor(biasf[:, 5:5 + KC], ps[:, 1, 0:KC], bias[:, 5:5 + KC], ALU.add)\
                       .then_inc(bias_ready, 1)
            dve.wait_ge(raw_loaded, 16 * sum(RAWS))
            raw2 = raw[:, :, :].rearrange("p a n -> p (a n)")[:, 0:KC * C].rearrange("p (k n) -> p k n", n=C)
            dve.tensor_copy(w2[:, :, 0, :], raw2[:, :, 0:A])
            dve.tensor_copy(w2[:, :, 3, 0:B], raw2[:, :, A:C])
            dve.tensor_copy(w2[:, :, 2, 0:B], raw2[:, :, A:C]).then_inc(w_hi, 1)
            dve.wait_ge(w_hi, 4)
            dve.tensor_tensor(w2[:, :, 1, :], raw2[:, :, 0:A], w2[:, :, 0, :].bitcast(F32), ALU.subtract)
            dve.tensor_tensor(w2[:, :, 2, B:128], raw2[:, :, A:C], w2[:, :, 2, 0:B].bitcast(F32), ALU.subtract)\
               .then_inc(w_lo, 1)
            dve.wait_ge(bias_ready, 2)
            low_parts(T1, zh1, zl1, zh1_done, zl1_done, 0)
            stats1(1, 1)

            def scores(i, pairs):
                wait(dve, pt_done, PAIRS, i - 1, PAIRS)
                for p in pairs:
                    s = ps[:, S[p], 0:HEADS * TOK].rearrange("p (h k) -> p h k", k=TOK)
                    wait(dve, s_done, PAIRS, i, p + 1)
                    dve.tensor_reduce(mx[:, p, :], s, AX.X, ALU.max).then_inc(smax, 1)
                    wait(dve, smax, PAIRS, i, p + 1)
                    dve.tensor_tensor(prob[:, p, :, 0:TOK], s,
                                      mx[:, p, :].unsqueeze(2).broadcast_to([128, HEADS, TOK]), ALU.subtract)\
                       .then_inc(s_sub, 1)

            def hidden(prev, m):
                wait(dve, g_done, KC, prev, m + 1)
                wait(dve, y_done, 2, prev - 1, 2)
                dve.tensor_copy(gh[:, m, :], g[:, m, :]).then_inc(gh_ready, 1)

            def residual(half, bank, src, dst, add_done):
                dve.tensor_tensor(dst[:, 2 * half:2 * half + 2, :],
                                  ps[:, bank, :].rearrange("p (q n) -> p q n", n=256)[:, :, 0:C],
                                  src[:, 2 * half:2 * half + 2, :], ALU.add).then_inc(add_done, 1)

            def result(prev, parity, half):
                if half == 0:
                    wait(dve, stored[parity], 16 * MOVES, prev // 2, 0)
                wait(dve, ty_done, 2, prev, half + 1)
                residual(half, TY[half], x2, yo[:, parity, :, :], yo_done)

            def row_sums(i, half):
                wait(dve, p_exp, 2, i, half + 1)
                pairs = slice(2 * half, 2 * half + 2)
                dve.tensor_reduce(psum_row[:, pairs, :], prob[:, pairs, :, 0:TOK], AX.X, ALU.add).then_inc(p_sum, 1)
                wait(dve, p_sum, 2, i, half + 1)
                dve.reciprocal(rcp[:, pairs, :], psum_row[:, pairs, :]).then_inc(p_rcp, 1)

            def body(i, parity):
                prev = i - 1
                if attends(i):
                    scores(i, (0, 1))
                if feeds(i):
                    low_parts(T2, zh2, zl2, zh2_done, zl2_done, prev)
                if attends(i):
                    scores(i, (2, 3))
                if more(i):
                    apply1(i + 1, 1 - parity)
                if feeds(i):
                    for m in range(KC):
                        hidden(prev, m)
                if attends(i):
                    row_sums(i, 0)
                    row_sums(i, 1)
                if more(i):
                    low_parts(T1, zh1, zl1, zh1_done, zl1_done, i + 1)
                if attends(i):
                    wait(dve, oh_ready, 2, i, 1)
                    dve.scalar_tensor_tensor(windows(ol[:, :], TOK), windows(ps[:, PV[0], 0:N], TOK, EVEN),
                                             biasf[:, 3:4], windows(oh[:, 0, :], TOK).bitcast(F32),
                                             ALU.add, ALU.subtract).then_inc(ol_ready, 1)
                    wait(dve, oh_ready, 2, i, 2)
                    dve.scalar_tensor_tensor(windows(oh[64:128, 1, :], TOK), windows(ps[0:64, PV[1], 0:N], TOK, EVEN),
                                             biasf[0:64, 4:5], windows(oh[0:64, 1, :], TOK).bitcast(F32),
                                             ALU.add, ALU.subtract).then_inc(ol_ready, 1)
                if feeds(i):
                    result(prev, 1 - parity, 0)
                    result(prev, 1 - parity, 1)
                if attends(i):
                    wait(dve, xb_done, 1, i, 1)
                    wait(dve, yo_done, 2, i - 1, 2)
                    wait(dve, z2_done, 1, i - 1, 1)
                    for half in range(2):
                        wait(dve, proj_done, 2, i, half + 1)
                        residual(half, PROJ[half], xb, x2, x2_done)
                    wait(dve, x2_done, 2, i, 2)
                    norm_stats(x2, st2, mv2, bn2, mv2_done, i)
                    if more(i + 1):
                        stats1(i + 2, parity)
                    wait(dve, t2_done, 1, i - 1, 1)
                    norm_apply(x2, mv2, rs2, z2, i, mv2_done, rs2_done, z2_done)

            iterations(dve, body)

        @block.scalar
        def _(act):
            act.wait_ge(pads_ready, 1)
            act.wait_ge(bias_ready, 2)
            act.wait_ge(ident_ready, 2)

            def high_parts(bank, zh, t_done, hi_done, grp):
                stride, n = (WIDE, EVEN) if zh is zh1 else (TOK, TOK)
                wait(act, t_done, 1, grp, 1)
                act.activation(zh[:, :, :].rearrange("p a (w t) -> p a w t", t=stride)[:, :, :, 0:n],
                               ps[:, bank:bank + 2, :].rearrange("p a (w t) -> p a w t", t=WIDE)[:, :, :, 0:n],
                               ACT.Copy).then_inc(hi_done, 1)

            def queries_and_keys(grp):
                wait(act, s_done, PAIRS, grp - 1, PAIRS)
                wait(act, qk_done, 3, grp, 1)
                for h in range(4):
                    r = slice(32 * h, 32 * h + 32)
                    act.activation(kA[r, :, h, :], windows(ps[r, QK[1], 0:N], TOK, EVEN), ACT.Identity,
                                   bias=biasf[r, 1:2])
                wait(act, qk_done, 3, grp, 2)
                act.activation(qA[:, 0:N], ps[:, QK[0], 0:N], ACT.Identity, bias=biasf[:, 0:1])
                wait(act, qk_done, 3, grp, 3)
                for h in range(2):
                    r, s = slice(32 * h, 32 * h + 32), slice(64 + 32 * h, 96 + 32 * h)
                    act.activation(kB[r, :, h, :], windows(ps[s, QK[2], 0:N], TOK, EVEN), ACT.Identity,
                                   bias=biasf[s, 2:3])
                act.activation(qB[:, 0:N], ps[0:64, QK[2], 0:N], ACT.Identity, bias=biasf[0:64, 2:3])\
                   .then_inc(qk_ready, 1)

            def values(i):
                wait(act, v_done, 1, i, 1)
                wait(act, pv_done, 1, i - 1, 1)
                vps = ps[:, V:V + 2, :].rearrange("p b (q n) -> p (b q) n", n=256)
                for w in range(2):
                    for par in range(2):
                        src = vps[64 * w:64 * w + 64, :, 0:C].rearrange("p q (j e d) -> p q j e d", j=3, e=2)
                        last = act.activation(vd[64 * par:64 * par + 64, :, :, w, par, :], src[:, :, :, par, :],
                                              ACT.Copy)
                last.then_inc(v_ready, 1)

            high_parts(T1, zh1, t1_done, zh1_done, 0)
            queries_and_keys(0)

            def body(i, parity):
                prev = i - 1
                if attends(i):
                    values(i)
                if feeds(i):
                    wait(act, spare_done, 1, prev - 1, 1)
                    act.activation(spare[:, :], ident[0:1, 0:1], ACT.Gelu).then_inc(spare_done, 1)
                    wait(act, h_done, KC, prev - 1, KC)
                    high_parts(T2, zh2, t2_done, zh2_done, prev)
                    for m in range(KC):
                        wait(act, h_done, KC, prev, m + 1)
                        wait(act, gl_ready, KC, prev - 1, m + 1)
                        act.activation(g[:, m, :], ps[:, H[m], 0:M], ACT.Gelu, bias=biasf[:, 5 + m:6 + m])\
                           .then_inc(g_done, 1)
                if attends(i):
                    for half in range(2):
                        pairs = slice(2 * half, 2 * half + 2)
                        wait(act, s_sub, PAIRS, i, 2 * half + 2)
                        act.activation(prob[:, pairs, :, 0:TOK], prob[:, pairs, :, 0:TOK], ACT.Exp, scale=SCALE)\
                           .then_inc(p_exp, 1)
                if more(i):
                    wait(act, v_done, 1, i, 1)
                    high_parts(T1, zh1, t1_done, zh1_done, i + 1)
                if attends(i):
                    wait(act, pv_done, 1, i - 1, 1)
                    for p in range(PAIRS):
                        wait(act, pt_done, PAIRS, i, p + 1)
                        act.activation(pt[:, p, :, :, :],
                                       ps[:, TP[p], 0:384].rearrange("p (j w q) -> p j w q", j=3, w=2)[:, :, :, 0:TOK],
                                       ACT.Copy).then_inc(pt_ready, 1)
                if feeds(i):
                    for part in range(2):
                        wait(act, y_done, 2, prev, part + 1)
                        wait(act, ty_done, 2, prev - 1, 2)
                        act.activation(windows(yT[:, part, :], TOK), windows(ps[:, Y[part], 0:M], TOK, TOK),
                                       ACT.Identity, bias=b2[:, part:part + 1]).then_inc(yT_ready, 1)
                if attends(i):
                    wait(act, pv_done, 1, i, 1)
                    wait(act, proj_done, 2, i - 1, 2)
                    act.activation(windows(oh[:, 0, :], TOK), windows(ps[:, PV[0], 0:N], TOK, EVEN), ACT.Identity,
                                   bias=biasf[:, 3:4]).then_inc(oh_ready, 1)
                    act.activation(windows(oh[0:64, 1, :], TOK), windows(ps[0:64, PV[1], 0:N], TOK, EVEN), ACT.Identity,
                                   bias=biasf[0:64, 4:5]).then_inc(oh_ready, 1)
                if more(i):
                    queries_and_keys(i + 1)

            iterations(act, body)

        @block.tensor
        def _(pe):
            pe.wait_ge(pads_ready, 1)
            pe.wait_ge(ident_ready, 2)
            pe.wait_ge(twice_ready, 3)
            pe.wait_ge(consts_loaded, 16 * NCONST)

            def transposes(bank, z, t_done):
                for p in range(PAIRS):
                    for part in range(2):
                        last = pe.transpose(ps[:, bank + part, 128 * p:128 * p + 128],
                                            z[:, p, 64 * part:64 * part + 128], ident[:, :])
                last.then_inc(t_done, 1)

            def offsets(bank, n, tiles):
                for col, (c0, m) in enumerate(tiles):
                    pe.matmul(ps[0:m, bank, col:col + 1], raw[:, 0, c0:c0 + m], lnb[:, n, 0:1], start=True, stop=False)
                    last = pe.matmul(ps[0:m, bank, col:col + 1], raw[0:64, 1, c0:c0 + m], lnb[0:64, n, 1:2],
                                     start=False, stop=True)
                last.then_inc(bias_mm, 1)

            pe.wait_ge(raw_loaded, 16 * RAWS[0])
            offsets(0, 0, [(128 * t, 128) for t in range(4)] + [(512, 64)])
            wait(pe, z1_done, 1, 0, 1)
            transposes(T1, z1, t1_done)
            pe.wait_ge(raw_loaded, 16 * (RAWS[0] + RAWS[1]))
            offsets(1, 1, [(128 * k, 128) for k in range(KC)])
            pe.wait_ge(w_lo, 4)
            pe.wait_ge(bias_ready, 2)

            def project(dst, zh, zl, w, cols, pair=None, waits={}):
                for n, (act_, part) in enumerate(((zh[:, 0, :], 0), (zh[:, 0, :], 1), (zl[:, :], 0),
                                                  (zh[:, 1, :], 2), (zh[:, 1, :], 3))):
                    for s, group, k in waits.get(n, ()):
                        wait(pe, s, 2, group, k)
                    if pair is None:
                        last = pe.matmul(dst, cols(w, part), act_ if zh is zh2 else windows(act_), start=(n == 0),
                                         stop=(n == 4))
                    else:
                        last = pe.matmul(dst, pair_of(act_, pair), cols(w, part), start=(n == 0), stop=(n == 4))
                return last

            def qk(i):
                wait(pe, zh1_done, 1, i, 1)
                wait(pe, zl1_done, 1, i, 1)
                wait(pe, ol_ready, 2, i - 1, 2)
                for t in (1, 0, 2):
                    project(ps[:, QK[t], 0:N], zh1, zl1, wqkv, lambda w, part: w[:, part, 128 * t:128 * t + 128])\
                        .then_inc(qk_done, 1)

            def v(i):
                wait(pe, x2_done, 2, i - 1, 1)
                for p in range(PAIRS):
                    last = project(ps[:, V + p // 2, 256 * (p % 2):256 * (p % 2) + C], zh1, zl1, wqkv,
                                   lambda w, part: w[:, part, 2 * C:3 * C], pair=p)
                last.then_inc(v_done, 1)

            def s(i, pairs):
                if 0 in pairs:
                    wait(pe, qk_ready, 1, i, 1)
                for p in pairs:
                    if p < 2:
                        wait(pe, yo_done, 2, i - 2, p + 1)
                    for w in range(2):
                        c0, r = (2 * p + w) * EVEN, slice(64 * w, 64 * w + 64)
                        pe.matmul(ps[r, S[p], 0:4 * TOK], qA[:, c0:c0 + WIDE],
                                  kA[:, 2 * p + w, :, :].rearrange("p h k -> p (h k)"), start=True, stop=True)
                        last = pe.matmul(ps[r, S[p], 4 * TOK:6 * TOK], qB[:, c0:c0 + WIDE],
                                         kB[:, 2 * p + w, :, :].rearrange("p h k -> p (h k)"), start=True, stop=True)
                    last.then_inc(s_done, 1)

            def mlp1(prev):
                wait(pe, zh2_done, 1, prev, 1)
                wait(pe, zl2_done, 1, prev, 1)
                for m in range(KC):
                    if m < 2 and attends(prev + 1):
                        wait(pe, s_sub, PAIRS, prev + 1, m + 1)
                    if m == 4 and attends(prev + 1):
                        wait(pe, v_ready, 1, prev + 1, 1)
                    project(ps[:, H[m], 0:M], zh2, zl2, w1, lambda w, part: w[:, part, 128 * m:128 * m + 128])\
                        .then_inc(h_done, 1)

            def mlp2_high(prev):
                for part, halves in ((0, (0, 1)), (1, (2,))):
                    wait(pe, g_done, KC, prev, part + 1)
                    for k in range(KC):
                        wait(pe, gh_ready, KC, prev, k + 1)
                        for half in halves:
                            pe.matmul(ps[:, Y[part], 0:M], w2[:, k, half, :], gh[:, k, :],
                                      start=(k == 0 and half == halves[0]), stop=False)

            def mlp2_low(prev, part):
                for k in range(KC):
                    wait(pe, gl_ready, KC, prev, k + 1)
                    last = pe.matmul(ps[:, Y[part], 0:M], w2[:, k, 3 * part, :], gl[:, k, :], start=False,
                                     stop=(k == KC - 1))
                last.then_inc(y_done, 1)

            def turn_result(prev):
                wait(pe, yT_ready, 2, prev, 2)
                for p in range(PAIRS):
                    bank, c0 = TY[p // 2], 256 * (p % 2)
                    pe.transpose(ps[:, bank, c0:c0 + A], pair_of(yT[:, 0, :], p), ident[:, :])
                    last = pe.matmul(ps[:, bank, c0 + A:c0 + C], pair_of(yT[:, 1, :], p), twice[:, :], start=True,
                                     stop=True)
                    if p % 2:
                        last.then_inc(ty_done, 1)

            def turn_probs(i):
                for p in range(PAIRS):
                    wait(pe, p_norm, PAIRS, i, p + 1)
                    if p >= 2:
                        wait(pe, g_done, KC, i - 1, p + 1)
                    for j in range(3):
                        last = pe.transpose(ps[:, TP[p], 128 * j:128 * j + 128],
                                            prob[:, p, 2 * j:2 * j + 2, :].rearrange("p h k -> p (h k)"), ident[:, :])
                    last.then_inc(pt_done, 1)

            def pv(i):
                wait(pe, v_ready, 1, i, 1)
                for p in range(PAIRS):
                    wait(pe, pt_ready, PAIRS, i, p + 1 if p else 2)
                    for w in range(2):
                        c0 = (2 * p + w) * EVEN
                        for j in range(3):
                            r = slice(64 * (j % 2), 64 * (j % 2) + 64)
                            last = pe.matmul(ps[r, PV[j // 2], c0:c0 + TOK],
                                             vd[:, p, j, w, :, :].rearrange("p e d -> p (e d)"),
                                             pt[:, p, j, w, :], start=True, stop=True)
                last.then_inc(pv_done, 1)

            def proj(i):
                if more(i):
                    wait(pe, zl1_done, 1, i + 1, 1)
                for p in range(PAIRS):
                    parts = {0: [(oh_ready, i, 1)], 2: [(ol_ready, i, 1)], 3: [(oh_ready, i, 2), (ol_ready, i, 2)]}
                    last = project(ps[:, PROJ[p // 2], 256 * (p % 2):256 * (p % 2) + C], oh, ol, wproj,
                                   lambda w, part: w[:, part, :], pair=p, waits=parts if p == 0 else {})
                    if p % 2:
                        last.then_inc(proj_done, 1)

            qk(0)

            def body(i, parity):
                prev = i - 1
                if attends(i):
                    v(i)
                    s(i, (0, 1))
                if feeds(i):
                    wait(pe, z2_done, 1, prev, 1)
                    wait(pe, x2_done, 2, prev, 2)
                    if attends(i):
                        wait(pe, qk_ready, 1, i, 1)
                    transposes(T2, z2, t2_done)
                if attends(i):
                    s(i, (2, 3))
                if feeds(i):
                    mlp1(prev)
                    mlp2_high(prev)
                    mlp2_low(prev, 0)
                if more(i):
                    wait(pe, z1_done, 1, i + 1, 1)
                    if feeds(i):
                        wait(pe, g_done, KC, prev, KC)
                    else:
                        wait(pe, v_ready, 1, i, 1)
                    transposes(T1, z1, t1_done)
                if attends(i):
                    turn_probs(i)
                if feeds(i):
                    mlp2_low(prev, 1)
                if attends(i):
                    pv(i)
                if feeds(i):
                    turn_result(prev)
                if attends(i):
                    proj(i)
                if more(i):
                    qk(i + 1)

            iterations(pe, body)


_INS = ["x"] + ["L0_conv_" + n for n in ("ln1_w", "ln1_b", "qkv_w", "qkv_b", "proj_w", "proj_b", "ln2_w", "ln2_b",
                                         "mlp_w1", "mlp_b1", "mlp_w2", "mlp_b2")]


def kernel(**inputs):
    import concourse.bacc as bacc
    from concourse.bass_utils import run_bass_kernel_spmd

    nc = bacc.Bacc("TRN2", target_bir_lowering=False, num_devices=1)
    arrays, args = {}, []
    for name in _INS:
        a = np.ascontiguousarray(inputs[name])
        arrays[f"in_{name}"] = a
        args.append(nc.dram_tensor(f"in_{name}", a.shape, mybir.dt.from_np(a.dtype), kind="ExternalInput").ap())
    out = nc.dram_tensor("out", (IMAGES, SIDE, SIDE, C), F32, kind="ExternalOutput").ap()
    swin_kernel(nc, *args, out)
    r = run_bass_kernel_spmd(nc, [arrays], core_ids=[0])
    return r.results[0]["out"]
```

```python
from contextlib import ExitStack

import numpy as np

import concourse.bass as bass
from concourse import mybir

ALU = mybir.AluOpType
ACT = mybir.ActivationFunctionType
AX = mybir.AxisListType
F32 = mybir.dt.float32
F32R = mybir.dt.float32r

IMAGES, SIDE, C = 16, 56, 192
WS, SHIFT, HEADS = 7, 3, 6
HD = C // HEADS
TOK = WS * WS
ROWS_W = SIDE // WS
GROUPS = IMAGES * ROWS_W
WIN = ROWS_W
PAIRS = WIN // 2
WIDE = 64
EVEN = TOK + 1
N = WIN * EVEN
PAIR = WIDE + TOK
M = WIN * TOK
COLS = WIN * WIDE
HID = 4 * C
KC = HID // 128
A, B = 128, C - 128
SCALE = float(HD) ** -0.5
EPS = 1e-5
GL_POOL = 4
PART = M // PAIRS
MOVES = 5


def swin_kernel(nc, x, ln1_w, ln1_b, qkv_w, qkv_b, proj_w, proj_b, ln2_w, ln2_b, mlp_w1, mlp_b1, mlp_w2,
                mlp_b2, out):
    with ExitStack() as ctx:
        def sb(name, shape, dt=F32):
            return ctx.enter_context(nc.sbuf_tensor(name, shape, dt))

        def sem(name):
            return ctx.enter_context(nc.semaphore(name))

        ident = sb("ident", [128, 128])
        raw_qkv = sb("raw_qkv", [128, 2, 3 * C])
        raw_proj = sb("raw_proj", [128, 2, C])
        raw_w1 = sb("raw_w1", [128, 2, HID])
        raw_w2 = sb("raw_w2", [128, KC, C])
        wqkv = sb("wqkv", [128, 4, 3 * C], F32R)
        wproj = sb("wproj", [128, 4, C], F32R)
        w1 = sb("w1", [128, 4, HID], F32R)
        w2 = sb("w2", [128, KC, 4, 128], F32R)
        lnw = sb("lnw", [128, 2, 2])
        lnb = sb("lnb", [128, 2, 2])
        bias = sb("bias", [128, 5 + KC])
        biasf = sb("biasf", [128, 5 + KC])
        projb = sb("projb", [PART, C])
        b2 = sb("b2", [128, 2])
        twice = sb("twice", [128, B])
        mhalf = sb("mhalf", [PART, PAIRS])
        eps = sb("eps", [PART, PAIRS])
        xin = sb("xin", [PART, 2, PAIRS, C])
        xb = sb("xb", [PART, PAIRS, C])
        st1 = sb("st1", [PART, PAIRS, 6])
        mv1 = sb("mv1", [PART, PAIRS, 2])
        ve1 = sb("ve1", [PART, PAIRS])
        rs1 = sb("rs1", [PART, PAIRS])
        z1 = sb("z1", [PART, PAIRS, C])
        zh1 = sb("zh1", [128, 2, COLS], F32R)
        zl1 = sb("zl1", [128, COLS], F32R)
        qA = sb("qA", [128, N + WIDE - EVEN])
        qB = sb("qB", [64, N + WIDE - EVEN])
        kA = sb("kA", [128, WIN, 4, TOK])
        kB = sb("kB", [64, WIN, 2, TOK])
        vd = sb("vd", [128, PAIRS, 3, 2, 2, HD])
        prob = sb("prob", [128, PAIRS, HEADS, 64])
        mx = sb("mx", [128, PAIRS, HEADS])
        psum_row = sb("psum_row", [128, PAIRS, HEADS])
        rcp = sb("rcp", [128, PAIRS, HEADS])
        pt = sb("pt", [128, PAIRS, 3, 2, TOK])
        oh = sb("oh", [128, 2, M], F32R)
        ol = sb("ol", [128, M], F32R)
        x2 = sb("x2", [PART, 2, PAIRS, C])
        st2 = sb("st2", [PART, PAIRS, 6])
        mv2 = sb("mv2", [PART, PAIRS, 2])
        ve2 = sb("ve2", [PART, PAIRS])
        rs2 = sb("rs2", [PART, PAIRS])
        z2 = sb("z2", [PART, PAIRS, C])
        zh2 = sb("zh2", [128, 2, M], F32R)
        zl2 = sb("zl2", [128, M], F32R)
        g = sb("g", [128, KC, M])
        gh = sb("gh", [128, KC, M], F32R)
        gl = sb("gl", [128, KC, M], F32R)
        yT = sb("yT", [128, 2, M])
        yo = sb("yo", [PART, 2, PAIRS, C])
        spare = sb("spare", [1, 1])

        ps = ctx.enter_context(nc.psum_tensor("ps", [128, 8, 512], F32))
        QK = (0, 1, 6)
        V = 3
        S = (5, 2, 0, 1)
        T2 = 6
        H = (5, 2, 7, 6, 3, 4)
        Y = (5, 2)
        TY = (5, 2)
        T1 = 3
        TP = (0, 1, 7, 6)
        PV = (0, 1)
        PROJ = (3, 7)
        OFFSETS = (5, 7)

        ln1_loaded = sem("ln1_loaded")
        consts_loaded = sem("consts_loaded")
        weight_loaded = [sem(f"{w}_loaded") for w in ("qkv", "proj", "w1", "w2")]
        ident_ready = sem("ident_ready")
        twice_ready = sem("twice_ready")
        scaled = sem("scaled")
        w_hi = sem("w_hi")
        w_lo = sem("w_lo")
        bias_mm = sem("bias_mm")
        bias_ready = sem("bias_ready")
        zeroed = sem("zeroed")
        pads_ready = sem("pads_ready")
        eps_ready = sem("eps_ready")
        x_loaded = [sem("x_loaded0"), sem("x_loaded1")]
        stored = [sem("stored0"), sem("stored1")]
        bn1, mv1_done, ve1_done, rs1_done, z1_done = map(sem, ("bn1", "mv1_done", "ve1_done", "rs1_done", "z1_done"))
        bn2, mv2_done, ve2_done, rs2_done, z2_done = map(sem, ("bn2", "mv2_done", "ve2_done", "rs2_done", "z2_done"))
        xb_done = sem("xb_done")
        t1_done, zh1_done, zl1_done = map(sem, ("t1_done", "zh1_done", "zl1_done"))
        t2_done, zh2_done, zl2_done = map(sem, ("t2_done", "zh2_done", "zl2_done"))
        qk_done = sem("qk_done")
        v_done = sem("v_done")
        qk_ready = sem("qk_ready")
        v_ready = sem("v_ready")
        s_done = sem("s_done")
        smax = sem("smax")
        s_sub = sem("s_sub")
        p_exp = sem("p_exp")
        p_sum = sem("p_sum")
        p_rcp = sem("p_rcp")
        p_norm = [sem("p_norm_pool"), sem("p_norm_dve")]
        pt_done = sem("pt_done")
        pt_ready = sem("pt_ready")
        pv_done = sem("pv_done")
        spare_done = sem("spare_done")
        oh_ready = sem("oh_ready")
        ol_ready = sem("ol_ready")
        proj_done = sem("proj_done")
        x2_done = sem("x2_done")
        h_done = sem("h_done")
        g_done = sem("g_done")
        gh_ready = sem("gh_ready")
        gl_ready = [sem("gl_ready_pool"), sem("gl_ready_dve")]
        y_done = sem("y_done")
        yT_ready = sem("yT_ready")
        ty_done = sem("ty_done")
        yo_done = sem("yo_done")

        def wait(eng, s, per_group, group, k):
            v = group * per_group + k
            if not isinstance(v, int) or v > 0:
                eng.wait_ge(s, v)

        def span(p):
            return slice(PART * p, PART * (p + 1))

        def windows(cols, stride, n):
            return cols.rearrange("p (w t) -> p w t", t=stride)[:, :, 0:n]

        def in_windows(cols, stride):
            return cols.rearrange("p (w t) -> p w t", t=stride)[:, :, 0:TOK]\
                       .rearrange("p w (r c) -> p w r c", c=WS)

        def in_rows(cols):
            return cols.rearrange("p (r w c) -> p w r c", r=WS, w=WIN)

        def views(bank):
            if bank == T1:
                return in_rows, lambda cols: in_windows(cols, WIDE)
            return lambda cols: cols, lambda cols: cols

        def half_rows(cols, half):
            return cols.rearrange("p (r c) -> p r c", r=WS)[:, :, SIDE // 2 * half:SIDE // 2 * (half + 1)]

        def outputs(half, part):
            return ps[:, PV[half], part * M // 2:(part + 1) * M // 2].rearrange("p (r c) -> p r c", r=WS)

        def moves(image_rows, win_row):
            top = (image_rows * SIDE + win_row * WS + SHIFT) * SIDE
            low = (image_rows * SIDE + ((win_row + 1) % ROWS_W) * WS) * SIDE
            turn = (WS - SHIFT) * SIDE - SHIFT
            for lo, hi, src in ((0, turn, top + SHIFT), (turn, M - SHIFT, low), (M - SHIFT, M, top)):
                while lo < hi:
                    blk, at = divmod(lo, PART)
                    whole = 0 if at else (hi - lo) // PART
                    n, blocks = (PART, whole) if whole else (min(hi - lo, PART - at), 1)
                    yield at, n, slice(blk, blk + blocks), src * C, [[C, n], [PART * C, blocks], [1, C]]
                    lo += n * blocks
                    src = src + n * blocks

        def iterations(eng, body, last=GROUPS - 4):
            for i in range(3):
                body(i, i % 2)
            with eng.Fori(0, (last - 2) // 2) as j:
                body(j * 2 + 3, 1)
                body(j * 2 + 4, 0)
            for i in range(last + 1, GROUPS + 1):
                body(i, i % 2)

        def attends(i):
            return not isinstance(i, int) or i < GROUPS

        def feeds(i):
            return not isinstance(i, int) or i > 0

        def more(i):
            return not isinstance(i, int) or i < GROUPS - 1

        def normalise(eng, i, half):
            wait(eng, p_rcp, 2, i, half + 1)
            for p in (2 * half, 2 * half + 1):
                eng.tensor_tensor(prob[:, p, :, 0:TOK], prob[:, p, :, 0:TOK],
                                  rcp[:, p, :].unsqueeze(2).broadcast_to([128, HEADS, TOK]), ALU.mult)\
                   .then_inc(p_norm[half], 1)

        def hidden_low(eng, prev, m):
            wait(eng, gh_ready, KC, prev, m + 1)
            wait(eng, y_done, 2, prev - 1, 2)
            own, n = (1, KC - GL_POOL) if m >= GL_POOL else (0, GL_POOL)
            eng.tensor_tensor(gl[:, m, :], g[:, m, :], gh[:, m, :].bitcast(F32), ALU.subtract).then_inc(gl_ready[own], 1)

        def wait_hidden_low(eng, prev, m):
            if m < GL_POOL:
                wait(eng, gl_ready[0], GL_POOL, prev, m + 1)
            else:
                wait(eng, gl_ready[1], KC - GL_POOL, prev, m + 1 - GL_POOL)

        QKV_ORDER = ((0, A, 0), (C, A, A), (A, B, 2 * A), (C + A, B, 2 * A + B), (2 * C, C, 2 * C))
        QKV, PROJ_W, W1, W2 = range(4)
        LOADS = (2, 2, 2, 1)
        NLN1, NCONST = 9, 7 + KC
        Q0, K0, V0, QK1, V1, HID0 = range(6)

        block = ctx.enter_context(nc.Block())

        @block.sync
        def _(sp):
            def small(dst, v, lo, shape, loaded):
                sp.dma_start(dst, bass.AP(v.tensor, v.offset + lo, shape)).then_inc(loaded, 16)

            def load_norm(n, w, b, loaded):
                for v, dst in ((w, lnw), (b, lnb)):
                    small(dst[:, n, 0:1], v, 0, [[1, A], [1, 1]], loaded)
                    small(dst[:, n, 1:2], v, A, [[0, 2], [1, B], [1, 1]], loaded)

            def load_x(g_row, win_row, parity):
                for p0, np_, blocks, off, ap in moves(g_row, win_row):
                    sp.dma_start(xin[p0:p0 + np_, parity, blocks, :], bass.AP(x.tensor, off, ap))\
                      .then_inc(x_loaded[parity], 16)

            def load_weight(n, raw, w):
                sp.dma_start(raw[:, 0, :], w[0:A, :]).then_inc(weight_loaded[n], 16)
                cols = w.shape[1]
                sp.dma_start(raw[:, 1, :], bass.AP(w.tensor, w.offset + A * cols, [[0, 2], [cols, B], [1, cols]]))\
                  .then_inc(weight_loaded[n], 16)

            load_x(0, 0, 0)
            load_weight(QKV, raw_qkv, qkv_w)
            load_norm(0, ln1_w, ln1_b, ln1_loaded)
            for col, lo in ((Q0, 0), (K0, C), (V0, 2 * C)):
                small(bias[:, col:col + 1], qkv_b, lo, [[1, A], [1, 1]], ln1_loaded)
            small(bias[:, QK1:QK1 + 1], qkv_b, A, [[C, 2], [1, B], [1, 1]], ln1_loaded)
            small(bias[0:B, V1:V1 + 1], qkv_b, 2 * C + A, [[1, B], [1, 1]], ln1_loaded)
            small(projb[:, :], proj_b, 0, [[0, PART], [1, C]], consts_loaded)
            load_x(0, 1, 1)
            load_weight(PROJ_W, raw_proj, proj_w)
            load_weight(W1, raw_w1, mlp_w1)
            load_norm(1, ln2_w, ln2_b, consts_loaded)
            for k in range(KC):
                small(bias[:, HID0 + k:HID0 + k + 1], mlp_b1, 128 * k, [[1, 128], [1, 1]], consts_loaded)
            small(b2[:, 0:1], mlp_b2, 0, [[1, A], [1, 1]], consts_loaded)
            small(b2[0:B, 1:2], mlp_b2, A, [[1, B], [1, 1]], consts_loaded)
            sp.dma_start(raw_w2[:, :, :], mlp_w2.rearrange("(k p) n -> p k n", p=128))\
              .then_inc(weight_loaded[W2], 16)

            def body(i, parity):
                if not isinstance(i, int) or i < GROUPS - 2:
                    nxt = i + 2
                    wait(sp, z1_done, 1, i, 1)
                    wait(sp, xb_done, 1, i, 1)
                    load_x((nxt // ROWS_W), nxt % ROWS_W, parity)
                if feeds(i):
                    prev = i - 1
                    wait(sp, yo_done, 2, prev, 2)
                    for p0, np_, blocks, off, ap in moves(prev // ROWS_W, prev % ROWS_W):
                        sp.dma_start(bass.AP(out.tensor, off, ap), yo[p0:p0 + np_, 1 - parity, blocks, :])\
                          .then_inc(stored[1 - parity], 16)

            iterations(sp, body)
            sp.wait_ge(stored[0], 16 * MOVES * (GROUPS // 2))
            sp.wait_ge(stored[1], 16 * MOVES * (GROUPS // 2))




        @block.gpsimd
        def _(pool):
            pool.memset(ident[:, :], 0.0).then_inc(ident_ready, 1)
            pool.memset(twice[:, :], 0.0).then_inc(twice_ready, 1)
            pool.wait_ge(ident_ready, 1)
            pool.affine_select(out=ident[:, :], in_=ident[:, :], compare_op=ALU.not_equal, fill=1.0, base=0,
                               pattern=[[-1, 128]], channel_multiplier=1).then_inc(ident_ready, 1)
            for n in range(2):
                pool.wait_ge(twice_ready, n + 1)
                pool.affine_select(out=twice[:, :], in_=twice[:, :], compare_op=ALU.not_equal, fill=1.0, base=-B * n,
                                   pattern=[[-1, B]], channel_multiplier=1).then_inc(twice_ready, 1)
            for t in (zh1[:, 0, :], zh1[:, 1, :], zl1[:, :]):
                pool.memset(t.bitcast(F32).rearrange("p (w t) -> p w t", t=WIDE)[:, :, TOK:WIDE], 0.0)
            pool.memset(qA[:, N:], 0.0)
            pool.memset(qB[:, N:], 0.0).then_inc(pads_ready, 1)
            pool.memset(mhalf[:, :], -0.5)
            pool.memset(eps[:, :], EPS).then_inc(eps_ready, 1)
            pool.memset(vd[:], 0.0)
            pool.memset(prob[:, :, :, TOK:], 0.0)
            pool.memset(w2[:, :, 3, B:128].bitcast(F32), 0.0).then_inc(pads_ready, 1)
            pool.wait_ge(eps_ready, 1)

            def add_proj_bias(grp, parity):
                wait(pool, x_loaded[parity], 16 * MOVES, grp // 2, 16 * MOVES)
                wait(pool, x2_done, 2, grp - 1, 2)
                pool.tensor_tensor(xb[:, :, :], xin[:, parity, :, :],
                                   projb[:, :].unsqueeze(1).broadcast_to([PART, PAIRS, C]), ALU.add)\
                    .then_inc(xb_done, 1)

            def rstd(mv, ve, rs, mv_done, ve_done, rs_done, grp, used):
                wait(pool, mv_done, 1, grp, 1)
                wait(pool, used, 1, grp - 1, 1)
                pool.tensor_tensor(ve[:, :], mv[:, :, 1], eps[:, :], ALU.add).then_inc(ve_done, 1)
                wait(pool, ve_done, 1, grp, 1)
                pool.tensor_tensor(rs[:, :], ve[:, :], mhalf[:, :], ALU.pow).then_inc(rs_done, 1)

            rstd(mv1, ve1, rs1, mv1_done, ve1_done, rs1_done, 0, z1_done)
            pool.wait_ge(consts_loaded, 16 * NCONST)
            add_proj_bias(0, 0)
            rstd(mv1, ve1, rs1, mv1_done, ve1_done, rs1_done, 1, z1_done)

            def body(i, parity):
                prev = i - 1
                if feeds(i):
                    for m in range(GL_POOL):
                        hidden_low(pool, prev, m)
                if attends(i):
                    normalise(pool, i, 0)
                    if more(i + 1):
                        rstd(mv1, ve1, rs1, mv1_done, ve1_done, rs1_done, i + 2, z1_done)
                    rstd(mv2, ve2, rs2, mv2_done, ve2_done, rs2_done, i, z2_done)
                if more(i):
                    add_proj_bias(i + 1, 1 - parity)

            iterations(pool, body)

        @block.vector
        def _(dve):
            dve.memset(b2[B:128, 1:2], 0.0)
            dve.memset(kA[:], 0.0)
            dve.memset(kB[:], 0.0).then_inc(zeroed, 1)

            def norm_stats(src, st, mv, bn, mv_done, grp):
                for p in range(PAIRS):
                    last = dve.bn_stats(st[:, p, :], src[:, p, :])
                last.then_inc(bn, 1)
                wait(dve, bn, 1, grp, 1)
                dve.nop(nofuse=True)
                for p in range(PAIRS):
                    last = dve.bn_aggr(mv[:, p, :], st[:, p, :])
                last.then_inc(mv_done, 1)

            def norm_apply(src, mv, rs, z, grp, mv_done, rs_done, z_done):
                wait(dve, rs_done, 1, grp, 1)
                wait(dve, mv_done, 1, grp, 1)
                for p in range(PAIRS):
                    last = dve.tensor_scalar(z[:, p, :], src[:, p, :], mv[:, p, 0:1], rs[:, p:p + 1],
                                             ALU.subtract, ALU.mult)
                last.then_inc(z_done, 1)

            def low_parts(bank, zh, zl, hi_done, lo_done, grp):
                take, put = views(bank)
                wait(dve, hi_done, 2, grp, 1)
                dve.tensor_tensor(put(zl[:, :]), take(ps[:, bank, 0:M]), put(zh[:, 0, :]).bitcast(F32), ALU.subtract)\
                   .then_inc(lo_done, 1)
                wait(dve, hi_done, 2, grp, 2)
                dve.tensor_tensor(put(zh[0:64, 1, :]), take(ps[64:128, bank + 1, 0:M]),
                                  put(zh[64:128, 1, :]).bitcast(F32), ALU.subtract).then_inc(lo_done, 1)

            def stats1(grp, parity):
                wait(dve, x_loaded[parity], 16 * MOVES, grp // 2, 16 * MOVES)
                wait(dve, z1_done, 1, grp - 1, 1)
                norm_stats(xin[:, parity, :, :], st1, mv1, bn1, mv1_done, grp)

            def apply1(grp, parity):
                wait(dve, t1_done, 1, grp - 1, 1)
                norm_apply(xin[:, parity, :, :], mv1, rs1, z1, grp, mv1_done, rs1_done, z1_done)

            def offset_bias(n, tiles):
                dve.wait_ge(bias_mm, n + 1)
                for p, cols in tiles:
                    last = dve.tensor_tensor(biasf[0:p, cols], ps[0:p, OFFSETS[n], cols], bias[0:p, cols], ALU.add)
                last.then_inc(bias_ready, 1)

            def low_weight(n, pieces):
                dve.wait_ge(w_hi, n + 1)
                for lo, raw, hi in pieces:
                    last = dve.tensor_tensor(lo, raw, hi.bitcast(F32), ALU.subtract)
                last.then_inc(w_lo, 1)

            stats1(0, 0)
            apply1(0, 0)
            dve.wait_ge(ln1_loaded, 16 * NLN1)
            offset_bias(0, ((128, slice(Q0, QK1 + 1)), (B, slice(V1, V1 + 1))))
            low_weight(QKV, [(wqkv[:, 2 * part + 1, to:to + n], raw_qkv[:, part, at:at + n],
                              wqkv[:, 2 * part, to:to + n]) for part in range(2) for at, n, to in QKV_ORDER])
            low_parts(T1, zh1, zl1, zh1_done, zl1_done, 0)
            stats1(1, 1)
            dve.wait_ge(consts_loaded, 16 * NCONST)
            offset_bias(1, ((128, slice(HID0, HID0 + KC)),))
            low_weight(PROJ_W, [(wproj[:, 2 * part + 1, :], raw_proj[:, part, :], wproj[:, 2 * part, :])
                                for part in range(2)])
            low_weight(W1, [(w1[:, 2 * part + 1, :], raw_w1[:, part, :], w1[:, 2 * part, :]) for part in range(2)])
            low_weight(W2, [(w2[:, :, 1, :], raw_w2[:, :, 0:A], w2[:, :, 0, :]),
                            (w2[:, :, 2, B:128], raw_w2[:, :, A:C], w2[:, :, 2, 0:B])])

            def scores(i, pairs):
                wait(dve, pt_done, PAIRS, i - 1, PAIRS)
                for p in pairs:
                    s = ps[:, S[p], 0:HEADS * TOK].rearrange("p (h k) -> p h k", k=TOK)
                    wait(dve, s_done, PAIRS, i, p + 1)
                    dve.tensor_reduce(mx[:, p, :], s, AX.X, ALU.max).then_inc(smax, 1)
                    wait(dve, smax, PAIRS, i, p + 1)
                    dve.tensor_tensor(prob[:, p, :, 0:TOK], s,
                                      mx[:, p, :].unsqueeze(2).broadcast_to([128, HEADS, TOK]), ALU.subtract)\
                       .then_inc(s_sub, 1)

            def hidden(prev, m):
                wait(dve, g_done, KC, prev, m + 1)
                wait(dve, y_done, 2, prev - 1, 2)
                dve.tensor_copy(gh[:, m, :], g[:, m, :]).then_inc(gh_ready, 1)

            def residual(half, bank, src, dst, add_done):
                dve.tensor_tensor(dst[:, 2 * half:2 * half + 2, :],
                                  ps[0:PART, bank, :].rearrange("p (q n) -> p q n", n=256)[:, :, 0:C],
                                  src[:, 2 * half:2 * half + 2, :], ALU.add).then_inc(add_done, 1)

            def result(prev, parity, half):
                if half == 0:
                    wait(dve, stored[parity], 16 * MOVES, prev // 2, 0)
                wait(dve, ty_done, 2, prev, half + 1)
                residual(half, TY[half], x2[:, parity, :, :], yo[:, parity, :, :], yo_done)

            def row_sums(i, half):
                wait(dve, p_exp, 2, i, half + 1)
                pairs = slice(2 * half, 2 * half + 2)
                dve.tensor_reduce(psum_row[:, pairs, :], prob[:, pairs, :, 0:TOK], AX.X, ALU.add).then_inc(p_sum, 1)
                wait(dve, p_sum, 2, i, half + 1)
                dve.reciprocal(rcp[:, pairs, :], psum_row[:, pairs, :]).then_inc(p_rcp, 1)

            def body(i, parity):
                prev = i - 1
                if attends(i):
                    scores(i, (0, 1))
                if feeds(i):
                    low_parts(T2, zh2, zl2, zh2_done, zl2_done, prev)
                if attends(i):
                    scores(i, (2, 3))
                if more(i):
                    apply1(i + 1, 1 - parity)
                if feeds(i):
                    for m in range(KC):
                        hidden(prev, m)
                        if m >= GL_POOL:
                            hidden_low(dve, prev, m)
                if attends(i):
                    row_sums(i, 0)
                    row_sums(i, 1)
                    normalise(dve, i, 1)
                if more(i + 1) and attends(i):
                    stats1(i + 2, parity)
                if more(i):
                    low_parts(T1, zh1, zl1, zh1_done, zl1_done, i + 1)
                if attends(i):
                    for half in range(2):
                        wait(dve, oh_ready, 4, i, 2 * half + 2)
                        dve.scalar_tensor_tensor(half_rows(ol[:, :], half), outputs(half, 0), biasf[:, V0:V0 + 1],
                                                 half_rows(oh[:, 0, :], half).bitcast(F32), ALU.add, ALU.subtract)\
                           .then_inc(ol_ready, 1)
                        dve.scalar_tensor_tensor(half_rows(oh[64:128, 1, :], half), outputs(half, 1)[0:64],
                                                 biasf[0:64, V1:V1 + 1], half_rows(oh[0:64, 1, :], half).bitcast(F32),
                                                 ALU.add, ALU.subtract).then_inc(ol_ready, 1)
                if attends(i):
                    wait(dve, xb_done, 1, i, 1)
                    wait(dve, yo_done, 2, i - 2, 2)
                    wait(dve, z2_done, 1, i - 1, 1)
                    for half in range(2):
                        wait(dve, proj_done, 2, i, half + 1)
                        residual(half, PROJ[half], xb, x2[:, parity, :, :], x2_done)
                    wait(dve, x2_done, 2, i, 2)
                    norm_stats(x2[:, parity, :, :], st2, mv2, bn2, mv2_done, i)
                if feeds(i):
                    result(prev, 1 - parity, 0)
                    result(prev, 1 - parity, 1)
                if attends(i):
                    wait(dve, t2_done, 1, i - 1, 1)
                    norm_apply(x2[:, parity, :, :], mv2, rs2, z2, i, mv2_done, rs2_done, z2_done)

            iterations(dve, body)

        @block.scalar
        def _(act):
            def high_parts(bank, zh, t_done, hi_done, grp):
                take, put = views(bank)
                wait(act, t_done, 1, grp, 1)
                act.activation(put(zh[:, 0, :]), take(ps[:, bank, 0:M]), ACT.Copy).then_inc(hi_done, 1)
                act.activation(put(zh[64:128, 1, :]), take(ps[64:128, bank + 1, 0:M]), ACT.Copy).then_inc(hi_done, 1)

            def heads_45(grp):
                wait(act, s_done, PAIRS, grp - 1, PAIRS)
                wait(act, qk_done, 3, grp, 1)
                for h in range(2):
                    r, s = slice(32 * h, 32 * h + 32), slice(64 + 32 * h, 96 + 32 * h)
                    act.activation(kB[r, :, h, :], windows(ps[s, QK[2], 0:N], EVEN, TOK), ACT.Identity,
                                   bias=biasf[s, QK1:QK1 + 1])
                act.activation(qB[:, 0:N], ps[0:64, QK[2], 0:N], ACT.Identity, bias=biasf[0:64, QK1:QK1 + 1])\
                   .then_inc(qk_ready, 1)

            def heads_0123(grp):
                wait(act, qk_done, 3, grp, 2)
                for h in range(4):
                    r = slice(32 * h, 32 * h + 32)
                    act.activation(kA[r, :, h, :], windows(ps[r, QK[1], 0:N], EVEN, TOK), ACT.Identity,
                                   bias=biasf[r, K0:K0 + 1])
                wait(act, qk_done, 3, grp, 3)
                act.activation(qA[:, 0:N], ps[:, QK[0], 0:N], ACT.Identity, bias=biasf[:, Q0:Q0 + 1])\
                   .then_inc(qk_ready, 1)

            def values(i):
                wait(act, v_done, 1, i, 1)
                wait(act, pv_done, 2, i - 1, 2)
                vps = ps[:, V:V + 2, :].rearrange("p b (q n) -> p (b q) n", n=256)
                for w in range(2):
                    for par in range(2):
                        src = vps[64 * w:64 * w + TOK, :, 0:C].rearrange("p q (j e d) -> p q j e d", j=3, e=2)
                        last = act.activation(vd[64 * par:64 * par + TOK, :, :, w, par, :], src[:, :, :, par, :],
                                              ACT.Copy)
                last.then_inc(v_ready, 1)

            def feature_result(prev, part):
                wait(act, y_done, 2, prev, part + 1)
                wait(act, ty_done, 2, prev - 1, 2)
                act.activation(yT[:, part, :], ps[:, Y[part], 0:M], ACT.Identity, bias=b2[:, part:part + 1])\
                   .then_inc(yT_ready, 1)

            def scale_weight(n, raw):
                act.wait_ge(bias_mm, n + 1)
                for part in range(2):
                    last = act.activation(raw[:, part, :], raw[:, part, :], ACT.Copy, scale=lnw[:, n, part:part + 1])
                last.then_inc(scaled, 1)
                act.wait_ge(scaled, n + 1)

            def high_weight(pieces):
                for hi, raw in pieces:
                    last = act.activation(hi, raw, ACT.Copy)
                last.then_inc(w_hi, 1)

            act.wait_ge(ln1_loaded, 16 * NLN1)
            scale_weight(0, raw_qkv)
            high_weight([(wqkv[:, 2 * part, to:to + n], raw_qkv[:, part, at:at + n])
                         for part in range(2) for at, n, to in QKV_ORDER])
            high_parts(T1, zh1, t1_done, zh1_done, 0)
            act.wait_ge(bias_ready, 1)
            act.wait_ge(zeroed, 1)
            heads_45(0)
            heads_0123(0)
            act.wait_ge(weight_loaded[PROJ_W], 16 * LOADS[PROJ_W])
            high_weight([(wproj[:, 2 * part, :], raw_proj[:, part, :]) for part in range(2)])
            act.wait_ge(consts_loaded, 16 * NCONST)
            scale_weight(1, raw_w1)
            high_weight([(w1[:, 2 * part, :], raw_w1[:, part, :]) for part in range(2)])
            act.wait_ge(weight_loaded[W2], 16 * LOADS[W2])
            high_weight([(w2[:, :, 0, :], raw_w2[:, :, 0:A]), (w2[:, :, 2, 0:B], raw_w2[:, :, A:C]),
                         (w2[:, :, 3, 0:B], raw_w2[:, :, A:C])])
            act.wait_ge(pads_ready, 2)
            act.wait_ge(bias_ready, 2)

            def body(i, parity):
                prev = i - 1
                if attends(i):
                    values(i)
                if feeds(i):
                    wait(act, h_done, KC, prev - 1, KC)
                    high_parts(T2, zh2, t2_done, zh2_done, prev)
                    wait(act, spare_done, 1, prev - 1, 1)
                    act.activation(spare[:, :], ident[0:1, 0:1], ACT.Gelu).then_inc(spare_done, 1)
                    for m in range(KC):
                        wait(act, h_done, KC, prev, m + 1)
                        wait_hidden_low(act, prev - 1, m)
                        act.activation(g[:, m, :], ps[:, H[m], 0:M], ACT.Gelu, bias=biasf[:, HID0 + m:HID0 + m + 1])\
                           .then_inc(g_done, 1)
                if attends(i):
                    for half in range(2):
                        pairs = slice(2 * half, 2 * half + 2)
                        wait(act, s_sub, PAIRS, i, 2 * half + 2)
                        act.activation(prob[:, pairs, :, 0:TOK], prob[:, pairs, :, 0:TOK], ACT.Exp, scale=SCALE)\
                           .then_inc(p_exp, 1)
                if feeds(i):
                    feature_result(prev, 0)
                if attends(i):
                    wait(act, pv_done, 2, i - 1, 2)
                    for p in range(PAIRS):
                        wait(act, pt_done, PAIRS, i, p + 1)
                        act.activation(pt[:, p, :, :, :],
                                       ps[:, TP[p], 0:384].rearrange("p (j w q) -> p j w q", j=3, w=2)[:, :, :, 0:TOK],
                                       ACT.Copy).then_inc(pt_ready, 1)
                if more(i):
                    wait(act, v_done, 1, i, 1)
                    high_parts(T1, zh1, t1_done, zh1_done, i + 1)
                if attends(i):
                    wait(act, proj_done, 2, i - 1, 2)
                    for half in range(2):
                        wait(act, pv_done, 2, i, half + 1)
                        act.activation(half_rows(oh[:, 0, :], half), outputs(half, 0), ACT.Identity, bias=biasf[:, V0:V0 + 1])\
                           .then_inc(oh_ready, 1)
                        act.activation(half_rows(oh[0:64, 1, :], half), outputs(half, 1)[0:64], ACT.Identity,
                                       bias=biasf[0:64, V1:V1 + 1]).then_inc(oh_ready, 1)
                if feeds(i):
                    feature_result(prev, 1)
                if more(i):
                    heads_45(i + 1)
                if more(i):
                    heads_0123(i + 1)

            iterations(act, body)

        @block.tensor
        def _(pe):
            def transposes(bank, z, t_done):
                for p in range(PAIRS):
                    for part in range(2):
                        last = pe.transpose(ps[:, bank + part, PART * p:PART * (p + 1)],
                                            z[:, p, 64 * part:64 * part + 128], ident[0:PART, 0:PART])
                last.then_inc(t_done, 1)

            def offsets(n, raw, tiles):
                for col, p0, c0, m in tiles:
                    dst = ps[p0:p0 + m, OFFSETS[n], col:col + 1]
                    pe.matmul(dst, raw[:, 0, c0:c0 + m], lnb[:, n, 0:1], start=True, stop=False)
                    last = pe.matmul(dst, raw[0:64, 1, c0:c0 + m], lnb[0:64, n, 1:2], start=False, stop=True)
                last.then_inc(bias_mm, 1)

            def project(dst, zh, zl, w, cols, tokens=None, passes=range(5), waits={}):
                operands = ((zh[:, 0, :], 0), (zh[:, 0, :], 1), (zl[:, :], 0), (zh[:, 1, :], 2), (zh[:, 1, :], 3))
                for n in passes:
                    act_, part = operands[n]
                    for s, per_group, group, k in waits.get(n, ()):
                        wait(pe, s, per_group, group, k)
                    if tokens is None:
                        last = pe.matmul(dst, cols(w, part), act_ if zh is zh2 else windows(act_, WIDE, EVEN), start=(n == 0),
                                         stop=(n == 4))
                    else:
                        last = pe.matmul(dst, act_[:, tokens], cols(w, part), start=(n == 0), stop=(n == 4))
                return last

            def qk(i, tiles):
                wait(pe, zh1_done, 2, i, 2)
                wait(pe, zl1_done, 2, i, 2)
                if tiles == (2,):
                    wait(pe, pt_ready, PAIRS, i - 1, PAIRS)
                else:
                    wait(pe, ol_ready, 4, i - 1, 4)
                for t in tiles:
                    project(ps[:, QK[t], 0:N], zh1, zl1, wqkv, lambda w, part: w[:, part, 128 * t:128 * t + 128])\
                        .then_inc(qk_done, 1)

            def v(i):
                wait(pe, x2_done, 2, i - 1, 1)
                for p in range(PAIRS):
                    last = project(ps[0:PAIR + 1, V + p // 2, 256 * (p % 2):256 * (p % 2) + C], zh1, zl1, wqkv,
                                   lambda w, part: w[:, part, 2 * C:3 * C], tokens=slice(2 * WIDE * p, 2 * WIDE * p + PAIR + 1))
                last.then_inc(v_done, 1)

            def s(i, pairs):
                if 0 in pairs:
                    wait(pe, qk_ready, 2, i, 2)
                for lo, n, q, k in ((0, 4, qA, kA), (4, 2, qB, kB)):
                    for p in pairs:
                        if lo == 0 and p < 2:
                            wait(pe, yo_done, 2, i - 2, p + 1)
                        for w in range(2):
                            c0, r = (2 * p + w) * EVEN, slice(64 * w, 64 * w + 64)
                            last = pe.matmul(ps[r, S[p], lo * TOK:(lo + n) * TOK], q[:, c0:c0 + WIDE],
                                             k[:, 2 * p + w, :, :].rearrange("p h k -> p (h k)"), start=True, stop=True)
                        if lo:
                            last.then_inc(s_done, 1)

            def mlp1(prev):
                def chunk(m, passes, waits={}):
                    return project(ps[:, H[m], 0:M], zh2, zl2, w1, lambda w, part: w[:, part, 128 * m:128 * m + 128],
                                   passes=passes, waits=waits)

                wait(pe, zh2_done, 2, prev, 1)
                for m in range(2):
                    if attends(prev + 1):
                        wait(pe, s_sub, PAIRS, prev + 1, m + 1)
                    chunk(m, (0, 1))
                for m in range(2):
                    chunk(m, (2,), {2: [(zl2_done, 2, prev, 1)]})
                for m in range(2):
                    chunk(m, (3, 4), {3: [(zh2_done, 2, prev, 2), (zl2_done, 2, prev, 2)]}).then_inc(h_done, 1)
                for m in range(2, KC):
                    if m == 4 and attends(prev + 1):
                        wait(pe, v_ready, 1, prev + 1, 1)
                    chunk(m, range(5)).then_inc(h_done, 1)

            def mlp2_high(prev):
                for part, halves in ((0, (0, 1)), (1, (2,))):
                    wait(pe, g_done, KC, prev, part + 1)
                    for k in range(KC):
                        wait(pe, gh_ready, KC, prev, k + 1)
                        for half in halves:
                            pe.matmul(ps[:, Y[part], 0:M], w2[:, k, half, :], gh[:, k, :],
                                      start=(k == 0 and half == halves[0]), stop=False)

            def mlp2_low(prev, part):
                for k in range(KC):
                    wait_hidden_low(pe, prev, k)
                    last = pe.matmul(ps[:, Y[part], 0:M], w2[:, k, 3 * part, :], gl[:, k, :], start=False,
                                     stop=(k == KC - 1))
                last.then_inc(y_done, 1)

            def turn_result(prev):
                wait(pe, yT_ready, 2, prev, 2)
                for p in range(PAIRS):
                    bank, c0 = TY[p // 2], 256 * (p % 2)
                    pe.transpose(ps[0:PART, bank, c0:c0 + A], yT[:, 0, span(p)], ident[:, :])
                    last = pe.matmul(ps[0:PART, bank, c0 + A:c0 + C], yT[:, 1, span(p)], twice[:, :], start=True,
                                     stop=True)
                    if p % 2:
                        last.then_inc(ty_done, 1)

            def turn_probs(i):
                for p in range(PAIRS):
                    wait(pe, p_norm[p // 2], 2, i, p % 2 + 1)
                    if p >= 2:
                        wait(pe, g_done, KC, i - 1, p + 1)
                    for j in range(3):
                        last = pe.transpose(ps[:, TP[p], 128 * j:128 * j + PAIR],
                                            prob[0:PAIR, p, 2 * j:2 * j + 2, :].rearrange("p h k -> p (h k)"),
                                            ident[0:PAIR, 0:PAIR])
                    last.then_inc(pt_done, 1)

            def pv(i):
                wait(pe, v_ready, 1, i, 1)
                for p in range(PAIRS):
                    wait(pe, pt_ready, PAIRS, i, p + 1)
                    for w in range(2):
                        for j in range(3):
                            r = slice(64 * (j % 2), 64 * (j % 2) + 64)
                            c0 = (2 * (p % 2) + w) * WS
                            last = pe.matmul(outputs(p // 2, j // 2)[r, :, c0:c0 + WS],
                                             vd[:, p, j, w, :, :].rearrange("p e d -> p (e d)"),
                                             pt[:, p, j, w, :], start=True, stop=True)
                    if p % 2:
                        last.then_inc(pv_done, 1)

            def proj(i):
                def block_of(p, passes, waits={}):
                    return project(ps[0:PART, PROJ[p // 2], 256 * (p % 2):256 * (p % 2) + C], oh, ol, wproj,
                                   lambda w, part: w[:, part, :], tokens=span(p), passes=passes, waits=waits)

                if more(i):
                    wait(pe, zl1_done, 2, i + 1, 2)
                if isinstance(i, int) and i == 0:
                    pe.wait_ge(w_lo, PROJ_W + 1)
                wait(pe, oh_ready, 4, i, 3)
                for p in range(PAIRS):
                    last = block_of(p, range(5), {} if p else {2: [(ol_ready, 4, i, 3)],
                                                               3: [(oh_ready, 4, i, 4), (ol_ready, 4, i, 4)]})
                    if p % 2:
                        last.then_inc(proj_done, 1)

            pe.wait_ge(weight_loaded[QKV], 16 * LOADS[QKV])
            pe.wait_ge(ln1_loaded, 16 * NLN1)
            offsets(0, raw_qkv, ((Q0, 0, 0, A), (K0, 0, C, A), (V0, 0, 2 * C, A), (QK1, 0, A, B),
                                 (QK1, B, C + A, B), (V1, 0, 2 * C + A, B)))
            pe.wait_ge(ident_ready, 2)
            wait(pe, z1_done, 1, 0, 1)
            transposes(T1, z1, t1_done)
            pe.wait_ge(pads_ready, 1)
            pe.wait_ge(w_lo, QKV + 1)
            qk(0, (2,))
            qk(0, (1, 0))
            pe.wait_ge(weight_loaded[W1], 16 * LOADS[W1])
            pe.wait_ge(consts_loaded, 16 * NCONST)
            offsets(1, raw_w1, [(HID0 + k, 0, 128 * k, 128) for k in range(KC)])
            pe.wait_ge(pads_ready, 2)
            pe.wait_ge(bias_ready, 2)

            def body(i, parity):
                prev = i - 1
                if attends(i):
                    v(i)
                    s(i, (0, 1))
                if feeds(i):
                    wait(pe, z2_done, 1, prev, 1)
                    wait(pe, x2_done, 2, prev, 2)
                    if attends(i):
                        wait(pe, qk_ready, 2, i, 2)
                    transposes(T2, z2, t2_done)
                if attends(i):
                    s(i, (2, 3))
                if feeds(i):
                    if isinstance(prev, int) and prev == 0:
                        pe.wait_ge(w_lo, W2 + 1)
                        pe.wait_ge(twice_ready, 3)
                    mlp1(prev)
                    mlp2_high(prev)
                    mlp2_low(prev, 0)
                if more(i):
                    wait(pe, z1_done, 1, i + 1, 1)
                    if feeds(i):
                        wait(pe, g_done, KC, prev, KC)
                    else:
                        wait(pe, v_ready, 1, i, 1)
                    transposes(T1, z1, t1_done)
                if attends(i):
                    turn_probs(i)
                if attends(i):
                    pv(i)
                if feeds(i):
                    mlp2_low(prev, 1)
                if more(i):
                    qk(i + 1, (2,))
                if attends(i):
                    proj(i)
                if feeds(i):
                    turn_result(prev)
                if more(i):
                    qk(i + 1, (1, 0))

            iterations(pe, body)


_INS = ["x"] + ["L0_conv_" + n for n in ("ln1_w", "ln1_b", "qkv_w", "qkv_b", "proj_w", "proj_b", "ln2_w", "ln2_b",
                                         "mlp_w1", "mlp_b1", "mlp_w2", "mlp_b2")]


def kernel(**inputs):
    import concourse.bacc as bacc
    from concourse.bass_utils import run_bass_kernel_spmd

    nc = bacc.Bacc("TRN2", target_bir_lowering=False, num_devices=1)
    arrays, args = {}, []
    for name in _INS:
        a = np.ascontiguousarray(inputs[name])
        arrays[f"in_{name}"] = a
        args.append(nc.dram_tensor(f"in_{name}", a.shape, mybir.dt.from_np(a.dtype), kind="ExternalInput").ap())
    out = nc.dram_tensor("out", (IMAGES, SIDE, SIDE, C), F32, kind="ExternalOutput").ap()
    swin_kernel(nc, *args, out)
    r = run_bass_kernel_spmd(nc, [arrays], core_ids=[0])
    return r.results[0]["out"]
```
